# Optimizing a Trainium2 kernel written in Bass

```python
import numpy as np
import jax
import jax.numpy as jnp

def _softmax(x, axis=-1):
    return jax.nn.softmax(x, axis=axis)

def _gelu(x):
    return jax.nn.gelu(x, approximate=True)

def _silu(x):
    return jax.nn.silu(x)

def _sigmoid(x):
    return jax.nn.sigmoid(x)

def _layernorm(x, axis=-1, eps=1e-05):
    m = jnp.mean(x, axis=axis, keepdims=True)
    v = jnp.var(x, axis=axis, keepdims=True)
    return (x - m) / jnp.sqrt(v + eps)

def _scatter_add(tgt, idx, src, axis=0):
    return tgt.at[idx].add(src)

def _segment_sum(src, seg, n):
    return jax.ops.segment_sum(src, seg, n)
kernel_name = 'mk_cond_resid_d4_seqx_r8_a958cb'

def setup_inputs(seed: int=0):
    np.random.seed(seed)
    _w = jnp.asarray

    def _rec_inputs():
        import jax
        import jax.numpy as jnp
        _rk = jax.random.key(seed)
        x = -7.109e-05 + 0.9999 * jax.random.normal(jax.random.fold_in(_rk, 1), (64, 32, 512), jnp.float32)
        _lenS = 32 - jax.random.randint(jax.random.fold_in(_rk, 7), (64,), 0, max(1, 32 // 4) + 1, jnp.int32)
        _lenS2 = 32 - jax.random.randint(jax.random.fold_in(_rk, 8), (64,), 0, max(1, 32 // 4) + 1, jnp.int32)
        itok_B_1_14 = jax.random.randint(jax.random.fold_in(_rk, 11), (64,), 1, 15, jnp.int32)
        itok_B_0_7 = jax.random.randint(jax.random.fold_in(_rk, 12), (64,), 0, 8, jnp.int32)
        itok_B_3_7 = jax.random.randint(jax.random.fold_in(_rk, 13), (64,), 3, 8, jnp.int32)
        itok_Bx16_0_63 = jax.random.randint(jax.random.fold_in(_rk, 14), (64, 16), 0, 64, jnp.int32)
        itok_B_207_1644 = jax.random.randint(jax.random.fold_in(_rk, 15), (64,), 207, 1645, jnp.int32)
        return (x, itok_B_1_14, itok_B_0_7, itok_B_3_7, itok_Bx16_0_63, itok_B_207_1644)
    x, itok_B_1_14, itok_B_0_7, itok_B_3_7, itok_Bx16_0_63, itok_B_207_1644 = _rec_inputs()

    def _L0_cond_setup():
        import jax, jax.numpy as jnp
        import numpy as np
        B, S, D_IN = (8, 256, 512)
        A, D_OUT = (16, 512)
        key = jax.random.key(seed)
        k1, k2, k3 = jax.random.split(key, 3)
        x = jax.random.normal(k1, (B, S, D_IN), dtype=jnp.float32)
        weight = jax.random.normal(k2, (A, D_OUT, D_IN), dtype=jnp.float32) * 0.02
        adapter_ids = jax.random.randint(k3, (B,), 0, A, dtype=jnp.int64)
        return {'x': x, 'weight': weight, 'adapter_ids': adapter_ids}
    _L0_cond_all = _L0_cond_setup()
    _L0_cond_in = {k: v for k, v in _L0_cond_all.items() if k in ('weight',)}
    del _L0_cond_all

    def _L1_cond_setup():
        import jax, jax.numpy as jnp
        import numpy as np
        TOP_K = 2
        LANG_BIAS = 5.0
        SCALING = 32.0 / 16.0
        LANGUAGE_PAD_ID = -1
        key = jax.random.key(seed)
        ks = jax.random.split(key, 6)
        B, T, D, O, E, R = (4, 256, 512, 512, 8, 16)
        x = jax.random.normal(ks[0], (B, T, D), dtype=jnp.float32)
        language_ids = jax.random.randint(ks[1], (B,), 0, E).astype(jnp.int64)
        W = jax.random.normal(ks[2], (O, D), dtype=jnp.float32) * (1.0 / np.sqrt(D))
        Wr = jax.random.normal(ks[3], (E, D), dtype=jnp.float32) * (1.0 / np.sqrt(D))
        A = jax.random.normal(ks[4], (E, R, D), dtype=jnp.float32) * (1.0 / np.sqrt(D))
        Bm = jax.random.normal(ks[5], (O, R), dtype=jnp.float32) * 0.0
        Bm = jnp.broadcast_to(Bm, (E, O, R)) + jax.random.normal(ks[5], (E, O, R), dtype=jnp.float32) * 0.02
        return {'x': x, 'language_ids': language_ids, 'W': W, 'Wr': Wr, 'A': A, 'B': Bm}
    _L1_cond_all = _L1_cond_setup()
    _L1_cond_in = {k: v for k, v in _L1_cond_all.items() if k in ('W', 'Wr', 'A', 'B')}
    del _L1_cond_all

    def _L2_cond_setup():
        import jax, jax.numpy as jnp
        import numpy as np
        MAX_LORAS, OUT, IN = (8, 512, 512)
        B, S = (4, 256)
        key = jax.random.key(seed)
        k1, k2, k3 = jax.random.split(key, 3)
        x = jax.random.normal(k1, (B, S, IN), dtype=jnp.float32)
        weight = jax.random.normal(k2, (MAX_LORAS, OUT, IN), dtype=jnp.float32) * 0.02
        adapter_ids = jax.random.randint(k3, (B,), 0, MAX_LORAS, dtype=jnp.int32)
        return {'x': x, 'weight': weight, 'adapter_ids': adapter_ids}
    _L2_cond_all = _L2_cond_setup()
    _L2_cond_in = {k: v for k, v in _L2_cond_all.items() if k in ('weight',)}
    del _L2_cond_all

    def _L3_cond_setup():
        import jax, jax.numpy as jnp
        import numpy as np
        B, S, HID = (4, 128, 512)
        D, HQ, HK = (128, 32, 8)
        PAGES, PSIZE, NPP = (64, 32, 16)
        THETA = 10000.0
        EPS = 1e-06
        SCALE = 1.0 / float(np.sqrt(D))

        def _rmsnorm(t, w):
            var = jnp.mean(t * t, axis=-1, keepdims=True)
            return t * jax.lax.rsqrt(var + EPS) * w

        def _rope(t, pos):
            inv_freq = 1.0 / THETA ** (jnp.arange(0, D, 2, dtype=jnp.float32) / D)
            freqs = pos[..., None].astype(jnp.float32) * inv_freq
            cos = jnp.cos(freqs)[:, :, None, :]
            sin = jnp.sin(freqs)[:, :, None, :]
            t1, t2 = (t[..., :D // 2], t[..., D // 2:])
            return jnp.concatenate([t1 * cos - t2 * sin, t2 * cos + t1 * sin], axis=-1)
        key = jax.random.key(seed)
        ks = jax.random.split(key, 10)
        x = jax.random.normal(ks[0], (B, S, HID), jnp.float32)
        Wq = jax.random.normal(ks[1], (HQ * D, HID), jnp.float32) * 0.02
        Wk = jax.random.normal(ks[2], (HK * D, HID), jnp.float32) * 0.02
        Wv = jax.random.normal(ks[3], (HK * D, HID), jnp.float32) * 0.02
        Wo = jax.random.normal(ks[4], (HID, HQ * D), jnp.float32) * 0.02
        q_norm_w = jax.random.uniform(ks[5], (D,), jnp.float32)
        k_norm_w = jax.random.uniform(ks[6], (D,), jnp.float32)
        k_cache = jax.random.normal(ks[7], (PAGES, PSIZE, HK, D), jnp.float32)
        v_cache = jax.random.normal(ks[8], (PAGES, PSIZE, HK, D), jnp.float32)
        block_table = jnp.arange(B * NPP, dtype=jnp.int32).reshape(B, NPP)
        cache_seqlens = jax.random.randint(ks[9], (B,), 0, 475).astype(jnp.int32)
        return dict(x=x, Wq=Wq, Wk=Wk, Wv=Wv, Wo=Wo, q_norm_w=q_norm_w, k_norm_w=k_norm_w, k_cache=k_cache, v_cache=v_cache, block_table=block_table, cache_seqlens=cache_seqlens)
    _L3_cond_all = _L3_cond_setup()
    _L3_cond_in = {k: v for k, v in _L3_cond_all.items() if k in ('Wq', 'Wk', 'Wv', 'Wo', 'q_norm_w', 'k_norm_w', 'k_cache', 'v_cache')}
    del _L3_cond_all
    return {'x': x, 'itok_B_1_14': itok_B_1_14, 'itok_B_0_7': itok_B_0_7, 'itok_B_3_7': itok_B_3_7, 'itok_Bx16_0_63': itok_Bx16_0_63, 'itok_B_207_1644': itok_B_207_1644, 'L0_cond_weight': _L0_cond_in['weight'], 'L1_cond_W': _L1_cond_in['W'], 'L1_cond_Wr': _L1_cond_in['Wr'], 'L1_cond_A': _L1_cond_in['A'], 'L1_cond_B': _L1_cond_in['B'], 'L2_cond_weight': _L2_cond_in['weight'], 'L3_cond_Wq': _L3_cond_in['Wq'], 'L3_cond_Wk': _L3_cond_in['Wk'], 'L3_cond_Wv': _L3_cond_in['Wv'], 'L3_cond_Wo': _L3_cond_in['Wo'], 'L3_cond_q_norm_w': _L3_cond_in['q_norm_w'], 'L3_cond_k_norm_w': _L3_cond_in['k_norm_w'], 'L3_cond_k_cache': _L3_cond_in['k_cache'], 'L3_cond_v_cache': _L3_cond_in['v_cache']}

def reference(x, itok_B_1_14, itok_B_0_7, itok_B_3_7, itok_Bx16_0_63, itok_B_207_1644, L0_cond_weight, L1_cond_W, L1_cond_Wr, L1_cond_A, L1_cond_B, L2_cond_weight, L3_cond_Wq, L3_cond_Wk, L3_cond_Wv, L3_cond_Wo, L3_cond_q_norm_w, L3_cond_k_norm_w, L3_cond_k_cache, L3_cond_v_cache):
    import jax
    import jax.numpy as jnp

    def _L0_cond_ref(x, weight, adapter_ids):
        import jax, jax.numpy as jnp
        import numpy as np
        B, S, D_IN = (8, 256, 512)
        A, D_OUT = (16, 512)
        w = weight[adapter_ids]
        return jnp.einsum('bij,bkj->bik', x, w)

    def _L1_cond_ref(x, language_ids, W, Wr, A, B):
        import jax, jax.numpy as jnp
        import numpy as np
        TOP_K = 2
        LANG_BIAS = 5.0
        SCALING = 32.0 / 16.0
        LANGUAGE_PAD_ID = -1
        base = jnp.einsum('btd,od->bto', x, W)
        E = Wr.shape[0]
        logits = jnp.einsum('btd,ed->bte', x.astype(jnp.float32), Wr.astype(jnp.float32))
        expert_targets = language_ids
        valid = expert_targets >= 0
        tgt = jnp.where(valid, expert_targets, 0)
        bias = jax.nn.one_hot(tgt, E, dtype=logits.dtype) * LANG_BIAS
        bias = jnp.where(valid[:, None], bias, 0.0)
        logits = logits + bias[:, None, :]
        topw, topi = jax.lax.top_k(logits, TOP_K)
        weights = jax.nn.softmax(topw, axis=-1)
        gates = jnp.sum(jax.nn.one_hot(topi, E, dtype=weights.dtype) * weights[..., None], axis=-2)
        gates = gates.astype(x.dtype)
        h = jnp.einsum('btd,erd->bter', x, A)
        lora_out = jnp.einsum('bter,bte,eor->bto', h, gates, B)
        return base + SCALING * lora_out

    def _L2_cond_ref(x, weight, adapter_ids):
        import jax, jax.numpy as jnp
        import numpy as np
        MAX_LORAS, OUT, IN = (8, 512, 512)
        B, S = (4, 256)
        w = weight[adapter_ids]
        return jnp.einsum('bsi,boi->bso', x, w)

    def _L3_cond_ref(x, Wq, Wk, Wv, Wo, q_norm_w, k_norm_w, k_cache, v_cache, block_table, cache_seqlens):
        import jax, jax.numpy as jnp
        import numpy as np
        B, S, HID = (4, 128, 512)
        D, HQ, HK = (128, 32, 8)
        PAGES, PSIZE, NPP = (64, 32, 16)
        THETA = 10000.0
        EPS = 1e-06
        SCALE = 1.0 / float(np.sqrt(D))

        def _rmsnorm(t, w):
            var = jnp.mean(t * t, axis=-1, keepdims=True)
            return t * jax.lax.rsqrt(var + EPS) * w

        def _rope(t, pos):
            inv_freq = 1.0 / THETA ** (jnp.arange(0, D, 2, dtype=jnp.float32) / D)
            freqs = pos[..., None].astype(jnp.float32) * inv_freq
            cos = jnp.cos(freqs)[:, :, None, :]
            sin = jnp.sin(freqs)[:, :, None, :]
            t1, t2 = (t[..., :D // 2], t[..., D // 2:])
            return jnp.concatenate([t1 * cos - t2 * sin, t2 * cos + t1 * sin], axis=-1)
        bsz, seqlen, _ = x.shape
        q = jnp.einsum('bsd,ed->bse', x, Wq).reshape(bsz, seqlen, HQ, D)
        k = jnp.einsum('bsd,ed->bse', x, Wk).reshape(bsz, seqlen, HK, D)
        v = jnp.einsum('bsd,ed->bse', x, Wv).reshape(bsz, seqlen, HK, D)
        q = _rmsnorm(q, q_norm_w)
        k = _rmsnorm(k, k_norm_w)
        pos = cache_seqlens[:, None] + jnp.arange(seqlen)[None, :]
        q = _rope(q, pos)
        k = _rope(k, pos)
        L = NPP * PSIZE
        kc = k_cache[block_table].reshape(bsz, L, HK, D)
        vc = v_cache[block_table].reshape(bsz, L, HK, D)
        k_all = jnp.concatenate([kc, k], axis=1)
        v_all = jnp.concatenate([vc, v], axis=1)
        valid_c = jnp.arange(L)[None, :] < cache_seqlens[:, None]
        valid = jnp.concatenate([valid_c, jnp.ones((bsz, seqlen), dtype=bool)], axis=1)
        rep = HQ // HK
        k_all = jnp.repeat(k_all, rep, axis=2)
        v_all = jnp.repeat(v_all, rep, axis=2)
        scores = jnp.einsum('bqhd,bkhd->bhqk', q, k_all) * SCALE
        scores = jnp.where(valid[:, None, None, :], scores, -1e+30)
        probs = jax.nn.softmax(scores, axis=-1)
        o = jnp.einsum('bhqk,bkhd->bqhd', probs, v_all)
        o = o.reshape(bsz, seqlen, HQ * D)
        return jnp.einsum('bse,de->bsd', o, Wo)
    x = x + _L0_cond_ref(x, L0_cond_weight, itok_B_1_14)
    x = x + _L1_cond_ref(x, itok_B_0_7, L1_cond_W, L1_cond_Wr, L1_cond_A, L1_cond_B)
    x = x + _L2_cond_ref(x, L2_cond_weight, itok_B_3_7)
    x = x + _L3_cond_ref(x, L3_cond_Wq, L3_cond_Wk, L3_cond_Wv, L3_cond_Wo, L3_cond_q_norm_w, L3_cond_k_norm_w, L3_cond_k_cache, L3_cond_v_cache, itok_Bx16_0_63, itok_B_207_1644)
    return x

_drawn_inputs = setup_inputs


def setup_inputs(seed=0):
    import zlib

    import numpy as np

    out = dict(_drawn_inputs(seed))
    spreads = {}
    factors = {'L1_cond_Wr': 3.996,
     'L3_cond_Wk': 29.01,
     'L3_cond_Wv': 38.177,
     'L3_cond_q_norm_w': 4.262,
     'L3_cond_k_norm_w': 28.119,
     'L3_cond_k_cache': 8.0,
     'L3_cond_v_cache': 8.0}
    for name, (base, spread) in spreads.items():
        noise = np.random.default_rng([zlib.crc32(name.encode()), seed]).standard_normal(out[name].shape)
        drawn = base * np.exp(spread * noise) if base else spread * noise
        out[name] = jnp.asarray(drawn.astype(out[name].dtype))
    for name, factor in factors.items():
        out[name] = (out[name] * factor).astype(out[name].dtype)
    return out
```

```python
import math
from contextlib import ExitStack

import numpy as np

import concourse.bass as bass
from concourse import mybir

F32 = mybir.dt.float32
F32R = mybir.dt.float32r
I32 = mybir.dt.int32
U32 = mybir.dt.uint32
ALU = mybir.AluOpType
ACT = mybir.ActivationFunctionType
AX = mybir.AxisListType
ds = bass.ds

P = 128
B, S, D = 64, 32, 512
T = B * S
KC = D // P
TILES = T // P
BPT = P // S
E, R = 8, 16
DH, HQ, HK = 128, 32, 8
G = HQ // HK
PAGES, PSIZE, NPP = 64, 32, 16
L = PAGES // BPT * PSIZE
THETA, EPS = 10000.0, 1e-6
SCALE = 1.0 / math.sqrt(DH)
LANG_BIAS, SCALING = 5.0, 2.0
MASKED = -1e30


class Scope:

    def __init__(self, nc):
        self.nc, self.ctx = nc, ExitStack()

    def __enter__(self):
        self.ctx.__enter__()
        return self

    def __exit__(self, *a):
        return self.ctx.__exit__(*a)

    def sb(self, name, shape, dt=F32):
        return self.ctx.enter_context(self.nc.sbuf_tensor(name, shape, dt))

    def ps(self, name, shape, dt=F32):
        return self.ctx.enter_context(self.nc.psum_tensor(name, shape, dt))

    def sem(self, name):
        return self.ctx.enter_context(self.nc.semaphore(name))

    def block(self):
        return self.ctx.enter_context(self.nc.Block())


def identity(nc, ident):
    with Scope(nc) as c:
        zeroed, made = c.sem("ident_zeroed"), c.sem("ident_made")
        block = c.block()

        @block.gpsimd
        def _(pool):
            nc.gpsimd.memset(ident[:], 0.0).then_inc(zeroed, 1)
            pool.wait_ge(zeroed, 1)
            nc.gpsimd.affine_select(out=ident[:], in_=ident[:], compare_op=ALU.not_equal, fill=1.0,
                                    base=0, pattern=[[-1, P]], channel_multiplier=1).then_inc(made, 1)
            pool.wait_ge(made, 1)


def load_x(nc, x, ident, XT):
    with Scope(nc) as c:
        nat = c.sb("x_nat", [P, 4, D])
        ps = c.ps("x_ps", [P, 2, D])
        loaded = [c.sem(f"x_loaded{s}") for s in range(4)]
        turned, kept = c.sem("x_turned"), c.sem("x_kept")
        tiles = x.rearrange("(t j) s d -> t (j s) d", j=BPT)
        block = c.block()

        @block.sync
        def _(sp):
            for t in range(4):
                sp.dma_start(nat[:, t, :], tiles[t]).then_inc(loaded[t], 16)
            with nc.sync.Fori(0, TILES // 4 - 1) as i:
                for s in range(4):
                    sp.wait_ge(turned, i * 4 + (s + 1))
                    sp.dma_start(nat[:, s, :], tiles[i * 4 + (s + 4)]).then_inc(loaded[s], 16)

        @block.tensor
        def _(pe):
            with nc.tensor.Fori(0, TILES // 4) as i:
                for s in range(4):
                    pe.wait_ge(loaded[s], i * 16 + 16)
                    pe.wait_ge(kept, i * 4 + (s + 1))
                    for k in range(KC):
                        last = nc.tensor.transpose(ps[:, s % 2, k * P:(k + 1) * P],
                                                   nat[:, s, k * P:(k + 1) * P], ident[:])
                    last.then_inc(turned, 1)

        @block.vector
        def _(dve):
            dve.sem_inc(kept, 2)
            with nc.vector.Fori(0, TILES // 4) as i:
                for s in range(4):
                    dve.wait_ge(turned, i * 4 + (s + 1))
                    nc.vector.tensor_copy(XT[:, ds(i * 4 + s, 1), :, :],
                                          ps[:, s % 2, :]).then_inc(kept, 1)


def transposed_weights(nc, ident, name, source, n, WT):
    with Scope(nc) as c:
        nat = c.sb(f"{name}_nat", [P, 2, KC, D])
        ps = c.ps(f"{name}_ps", [P, 2, KC, D])
        loaded = [c.sem(f"{name}_loaded{s}") for s in range(2)]
        turned = c.sem(f"{name}_turned")
        kept_dve, kept_act = c.sem(f"{name}_kept_dve"), c.sem(f"{name}_kept_act")
        block = c.block()

        @block.sync
        def _(sp):
            for s in range(2):
                sp.dma_start(nat[:, s, :, :], source(s)).then_inc(loaded[s], 16)
            with nc.sync.Fori(0, n // 2 - 1) as i:
                for s in range(2):
                    sp.wait_ge(turned, i * 2 + (s + 1))
                    sp.dma_start(nat[:, s, :, :], source(i * 2 + (s + 2))).then_inc(loaded[s], 16)

        @block.tensor
        def _(pe):
            with nc.tensor.Fori(0, n // 2) as i:
                for s in range(2):
                    pe.wait_ge(loaded[s], i * 16 + 16)
                    pe.wait_ge(kept_dve, i * 2 + (s + 1))
                    pe.wait_ge(kept_act, i * 2 + (s + 1))
                    for k in range(KC):
                        for o in range(KC):
                            last = nc.tensor.transpose(ps[:, s, k, o * P:(o + 1) * P],
                                                       nat[:, s, o, k * P:(k + 1) * P], ident[:])
                    last.then_inc(turned, 1)

        @block.vector
        def _(dve):
            dve.sem_inc(kept_dve, 2)
            with nc.vector.Fori(0, n // 2) as i:
                for s in range(2):
                    dve.wait_ge(turned, i * 2 + (s + 1))
                    nc.vector.tensor_copy(WT[:, ds(i * 2 + s, 1), 0:2, :], ps[:, s, 0:2, :]).then_inc(kept_dve, 1)

        @block.scalar
        def _(act):
            act.sem_inc(kept_act, 2)
            with nc.scalar.Fori(0, n // 2) as i:
                for s in range(2):
                    act.wait_ge(turned, i * 2 + (s + 1))
                    nc.scalar.copy(WT[:, ds(i * 2 + s, 1), 2:4, :], ps[:, s, 2:4, :]).then_inc(kept_act, 1)


def adapter_layer(nc, ident, name, weight, ids, n, x_in, x_out, XT):
    with Scope(nc) as outer:
        WT = outer.sb(f"{name}_WT", [P, n, KC, D])
        by_rows = weight.rearrange("a (o p) k -> a p o k", p=P)
        transposed_weights(nc, ident, f"{name}w", lambda a: by_rows[a], n, WT)

        with Scope(nc) as c:
            ids_sb = c.sb(f"{name}_ids", [1, B], I32)
            w_slot = c.sb(f"{name}_w_slot", [P, 2, BPT, D])
            x_slot = c.sb(f"{name}_x_slot", [P, 2, KC, P])
            x_row, y_row = c.sb(f"{name}_x_row", [P, 2, D]), c.sb(f"{name}_y_row", [P, 2, D])
            ps, psT = c.ps(f"{name}_ps", [P, 2, D]), c.ps(f"{name}_psT", [P, 2, D])
            ids_loaded = c.sem(f"{name}_ids_loaded")
            x_loaded = [c.sem(f"{name}_x_loaded{r}") for r in range(2)]
            stored = [c.sem(f"{name}_stored{r}") for r in range(2)]
            x_copied = c.sem(f"{name}_x_copied")
            w_dve, w_act = c.sem(f"{name}_w_dve"), c.sem(f"{name}_w_act")
            slots_free = c.sem(f"{name}_slots_free")
            added, turned, kept = c.sem(f"{name}_added"), c.sem(f"{name}_turned"), c.sem(f"{name}_kept")
            block = c.block()

            @block.sync
            def _(sp):
                sp.dma_start(ids_sb[:], ids.rearrange("(a b) -> a b", a=1)).then_inc(ids_loaded, 16)
                for r in range(2):
                    sp.sem_inc(stored[r], 16)
                    sp.dma_start(x_row[:, r, :], x_in[r]).then_inc(x_loaded[r], 16)

                def store(t, r):
                    sp.wait_ge(added, t + 1)
                    sp.dma_start(x_out[t], y_row[:, r, :]).then_inc(stored[r], 16)

                with nc.sync.Fori(0, TILES // 2 - 1) as i:
                    for r in range(2):
                        store(i * 2 + r, r)
                        sp.dma_start(x_row[:, r, :], x_in[i * 2 + (r + 2)]).then_inc(x_loaded[r], 16)
                for r in range(2):
                    store(TILES - 2 + r, r)
                for r in range(2):
                    sp.wait_ge(stored[r], 16 * (TILES // 2 + 1))

            @block.gpsimd
            def _(pool):
                for t in range(2):
                    nc.gpsimd.tensor_copy(x_slot[:, t, :, :], XT[:, t, :, :]).then_inc(x_copied, 1)
                with nc.gpsimd.Fori(1, TILES // 2) as i:
                    for r in range(2):
                        pool.wait_ge(slots_free, i * (2 * KC) + (KC * r - KC + 2))
                        nc.gpsimd.tensor_copy(x_slot[:, r, :, :], XT[:, ds(i * 2 + r, 1), :, :]).then_inc(x_copied, 1)

            def weights(eng, move, t, chunks, mine, sem):
                regs = {j: eng.value_load(ids_sb[0:1, ds(t * BPT + j, 1)], min_val=0, max_val=n - 1)
                        for j in sorted({j for k in chunks for j in mine[k % 2]})}
                for k in chunks:
                    eng.wait_ge(slots_free, t * KC + (k + 1))
                    for j in mine[k % 2]:
                        last = move(w_slot[:, k % 2, j, :], WT[:, ds(regs[j], 1), k, :])
                    last.then_inc(sem, 1)

            FIRST, SECOND = (0, 1), (2, 3)

            @block.scalar
            def _(act):
                mine = ((2, 3), (3,))
                act.sem_inc(kept, 2)
                act.wait_ge(ids_loaded, 16)

                def keep(t, r):
                    act.wait_ge(turned, t + 1)
                    nc.scalar.copy(XT[:, ds(t, 1), :, :], psT[:, r, :]).then_inc(kept, 1)

                weights(act, nc.scalar.copy, 0, FIRST + SECOND, mine, w_act)
                with nc.scalar.Fori(0, TILES // 2 - 1) as i:
                    for r in range(2):
                        weights(act, nc.scalar.copy, i * 2 + (r + 1), FIRST + SECOND, mine, w_act)
                        keep(i * 2 + r, r)
                weights(act, nc.scalar.copy, TILES - 1, FIRST + SECOND, mine, w_act)
                keep(TILES - 2, 0)
                keep(TILES - 1, 1)

            @block.vector
            def _(dve):
                mine = ((0, 1), (0, 1, 2))
                dve.wait_ge(ids_loaded, 16)

                def add(t, i, r):
                    dve.wait_ge(slots_free, t * KC + (KC + 2))
                    dve.wait_ge(x_loaded[r], i * 16 + 16)
                    dve.wait_ge(stored[r], i * 16 + 16)
                    nc.vector.tensor_tensor(y_row[:, r, :], ps[:, r, :], x_row[:, r, :], ALU.add).then_inc(added, 1)

                weights(dve, nc.vector.tensor_copy, 0, FIRST + SECOND, mine, w_dve)
                with nc.vector.Fori(0, TILES // 2 - 1) as i:
                    for r in range(2):
                        t = i * 2 + r
                        weights(dve, nc.vector.tensor_copy, t + 1, FIRST, mine, w_dve)
                        add(t, i, r)
                        weights(dve, nc.vector.tensor_copy, t + 1, SECOND, mine, w_dve)
                weights(dve, nc.vector.tensor_copy, TILES - 1, FIRST, mine, w_dve)
                add(TILES - 2, TILES // 2 - 1, 0)
                weights(dve, nc.vector.tensor_copy, TILES - 1, SECOND, mine, w_dve)
                add(TILES - 1, TILES // 2 - 1, 1)

            @block.tensor
            def _(pe):
                pe.sem_inc(slots_free, 2)

                def products(t, r):
                    pe.wait_ge(x_copied, t + 1)
                    for k in range(KC):
                        pe.wait_ge(w_dve, t * KC + (k + 1))
                        pe.wait_ge(w_act, t * KC + (k + 1))
                        for j in range(BPT):
                            rows = slice(j * S, (j + 1) * S)
                            last = nc.tensor.matmul(ps[rows, r, :], x_slot[:, r, k, rows], w_slot[:, k % 2, j, :],
                                                    start=k == 0, stop=k == KC - 1)
                        last.then_inc(slots_free, 1)

                def turn(t, r):
                    pe.wait_ge(added, t + 1)
                    pe.wait_ge(kept, t + 1)
                    for k in range(KC):
                        last = nc.tensor.transpose(psT[:, r, k * P:(k + 1) * P], y_row[:, r, k * P:(k + 1) * P],
                                                   ident[:])
                    last.then_inc(turned, 1)

                products(0, 0)
                with nc.tensor.Fori(0, TILES // 2 - 1) as i:
                    products(i * 2 + 1, 1)
                    turn(i * 2, 0)
                    products(i * 2 + 2, 0)
                    turn(i * 2 + 1, 1)
                products(TILES - 1, 1)
                turn(TILES - 2, 0)
                turn(TILES - 1, 1)


def expert_layer(nc, ident, W, Wr, A, Bm, ids, x_in, x_out, XT):
    ER = E * R
    with Scope(nc) as outer:
        WT = outer.sb("l1_WT", [P, KC, D])
        AT = outer.sb("l1_AT", [P, KC, ER + E])
        BT = outer.sb("l1_BT", [P, D])
        H = outer.sb("l1_H", [P, TILES, ER])
        HT = outer.sb("l1_HT", [P, TILES, P])
        logits = outer.sb("l1_logits", [P, TILES, E])
        lang = outer.sb("l1_lang", [P, TILES], I32)

        with Scope(nc) as c:
            Wn, An = c.sb("l1_Wn", [P, KC, D]), c.sb("l1_An", [P, D])
            Wrn, Bn = c.sb("l1_Wrn", [E, D]), c.sb("l1_Bn", [P, KC, ER])
            ps = c.ps("l1_wps", [P, 7, D])
            loaded, turned, kept = c.sem("l1_loaded"), c.sem("l1_turned"), c.sem("l1_kept")
            lang_loaded = c.sem("l1_lang_loaded")
            block = c.block()

            @block.sync
            def _(sp):
                sp.dma_start(Wn[:], W.rearrange("(o p) k -> p o k", p=P)).then_inc(loaded, 16)
                sp.dma_start(An[:], A.rearrange("e r k -> (e r) k")).then_inc(loaded, 16)
                sp.dma_start(Wrn[:], Wr).then_inc(loaded, 16)
                for o in range(KC):
                    sp.dma_start(Bn[:, o, :].rearrange("p (e r) -> p e r", e=E),
                                 Bm[:, o * P:(o + 1) * P, :].rearrange("e p r -> p e r")).then_inc(loaded, 16)
                by_tile = ids.rearrange("(t j) -> j t", j=BPT)
                for j in range(BPT):
                    sp.dma_start(lang[j * S:(j + 1) * S, :],
                                 by_tile[j:j + 1, :].broadcast_to([S, TILES]),
                                 allow_slow_non_contiguous=True).then_inc(lang_loaded, 16)
                sp.wait_ge(lang_loaded, 16 * BPT)

            @block.tensor
            def _(pe):
                pe.wait_ge(loaded, 16 * (3 + KC))
                for k in range(KC):
                    for o in range(KC):
                        nc.tensor.transpose(ps[:, k, o * P:(o + 1) * P], Wn[:, o, k * P:(k + 1) * P], ident[:])
                for k in range(KC):
                    nc.tensor.transpose(ps[:, 4, k * P:(k + 1) * P], An[:, k * P:(k + 1) * P], ident[:])
                for k in range(KC):
                    nc.tensor.transpose(ps[:, 5, k * E:(k + 1) * E], Wrn[:, k * P:(k + 1) * P], ident[0:E, 0:E])
                for o in range(KC):
                    last = nc.tensor.transpose(ps[:, 6, o * P:(o + 1) * P], Bn[:, o, :], ident[:])
                last.then_inc(turned, 1)

            @block.vector
            def _(dve):
                dve.wait_ge(turned, 1)
                nc.vector.tensor_copy(WT[:], ps[:, 0:KC, :])
                nc.vector.tensor_copy(AT[:, :, 0:ER], ps[:, 4, :].rearrange("p (k e) -> p k e", k=KC))
                nc.vector.tensor_copy(AT[:, :, ER:], ps[:, 5, 0:KC * E].rearrange("p (k e) -> p k e", k=KC))
                nc.vector.tensor_copy(BT[:], ps[:, 6, :]).then_inc(kept, 1)
                dve.wait_ge(kept, 1)

        with Scope(nc) as c:
            ps = c.ps("l1_hps", [P, 2, 512])
            done, banks_free = c.sem("l1_h_done"), c.sem("l1_h_free")
            block = c.block()

            @block.tensor
            def _(pe):
                for t in range(TILES):
                    pe.wait_ge(banks_free, t + 1)
                    for k in range(KC):
                        last = nc.tensor.matmul(ps[:, t % 2, 0:ER + E], XT[:, t, k, :], AT[:, k, :],
                                                start=k == 0, stop=k == KC - 1)
                    last.then_inc(done, 1)

            @block.vector
            def _(dve):
                dve.sem_inc(banks_free, 2)
                with nc.vector.Fori(0, TILES // 2) as i:
                    for r in range(2):
                        dve.wait_ge(done, i * 2 + (r + 1))
                        nc.vector.tensor_copy(logits[:, ds(i * 2 + r, 1), :], ps[:, r, ER:ER + E])
                        nc.vector.tensor_copy(H[:, ds(i * 2 + r, 1), :], ps[:, r, 0:ER]).then_inc(banks_free, 1)

        with Scope(nc) as c:
            iota = c.sb("l1_iota", [P, E])
            langf = c.sb("l1_langf", [P, TILES])
            hot = c.sb("l1_hot", [P, TILES, E])
            top, topi = c.sb("l1_top", [P, TILES, 8]), c.sb("l1_topi", [P, TILES, 8], U32)
            topf = c.sb("l1_topf", [P, TILES, 8])
            diff, ex, w1, w2 = (c.sb(f"l1_{x}", [P, TILES]) for x in ("diff", "ex", "w1", "w2"))
            g1, g2 = c.sb("l1_g1", [P, TILES, E]), c.sb("l1_g2", [P, TILES, E])
            chain, exp_done = c.sem("l1_chain"), c.sem("l1_exp")
            block = c.block()
            each = lambda x: x.unsqueeze(2).broadcast_to([P, TILES, E])
            iota_all = iota[:].unsqueeze(1).broadcast_to([P, TILES, E])

            @block.vector
            def _(dve):
                steps = [0]

                def link(ins):
                    steps[0] += 1
                    ins.then_inc(chain, 1)
                    dve.wait_ge(chain, steps[0])

                for e in range(E):
                    nc.vector.memset(iota[:, e:e + 1], float(e))
                link(nc.vector.tensor_copy(langf[:], lang[:]))
                link(nc.vector.tensor_tensor(hot[:], each(langf[:]), iota_all, ALU.is_equal))
                link(nc.vector.scalar_tensor_tensor(out=logits[:], in0=hot[:], scalar=LANG_BIAS, in1=logits[:],
                                                    op0=ALU.mult, op1=ALU.add))
                for t in range(TILES):
                    last = nc.vector.max(top[:, t, :], logits[:, t, :])
                link(last)
                for t in range(TILES):
                    last = nc.vector.max_index(topi[:, t, :], top[:, t, :], logits[:, t, :])
                link(last)
                nc.vector.tensor_copy(topf[:], topi[:])
                link(nc.vector.tensor_tensor(diff[:], top[:, :, 1], top[:, :, 0], ALU.subtract))
                dve.wait_ge(exp_done, 1)
                link(nc.vector.tensor_scalar(w1[:], ex[:], 1.0, None, ALU.add))
                link(nc.vector.reciprocal(w1[:], w1[:]))
                link(nc.vector.tensor_tensor(w2[:], ex[:], w1[:], ALU.mult))
                nc.vector.tensor_tensor(g1[:], each(topf[:, :, 0]), iota_all, ALU.is_equal)
                link(nc.vector.tensor_tensor(g2[:], each(topf[:, :, 1]), iota_all, ALU.is_equal))
                nc.vector.tensor_tensor(g1[:], g1[:], each(w1[:]), ALU.mult)
                link(nc.vector.tensor_tensor(g2[:], g2[:], each(w2[:]), ALU.mult))
                link(nc.vector.tensor_tensor(g1[:], g1[:], g2[:], ALU.add))
                link(nc.vector.tensor_scalar(g1[:], g1[:], SCALING, None, ALU.mult))
                h = H[:].rearrange("p t (e r) -> p (t e) r", r=R)
                gates = g1[:].rearrange("p t e -> p (t e)").unsqueeze(2).broadcast_to([P, TILES * E, R])
                link(nc.vector.tensor_tensor(h, h, gates, ALU.mult))

            @block.scalar
            def _(act):
                act.wait_ge(chain, 6)
                nc.scalar.activation(ex[:], diff[:], ACT.Exp).then_inc(exp_done, 1)

        with Scope(nc) as c:
            ps, psT = c.ps("l1_ps", [P, 2, D]), c.ps("l1_psT", [P, 4, D])
            x_row, y_row = c.sb("l1_x_row", [P, 2, D]), c.sb("l1_y_row", [P, 2, D])
            x_loaded = [c.sem(f"l1_x_loaded{r}") for r in range(2)]
            stored = [c.sem(f"l1_stored{r}") for r in range(2)]
            h_turned, h_kept = c.sem("l1_h_turned"), c.sem("l1_h_kept")
            done, added, turned, kept = (c.sem(f"l1_{x}") for x in ("done", "added", "turned", "kept"))
            block = c.block()

            @block.sync
            def _(sp):
                for t in range(2):
                    sp.dma_start(x_row[:, t, :], x_in[t]).then_inc(x_loaded[t], 16)
                for t in range(TILES):
                    sp.wait_ge(added, t + 1)
                    sp.dma_start(x_out[t], y_row[:, t % 2, :]).then_inc(stored[t % 2], 16)
                    if t + 2 < TILES:
                        sp.dma_start(x_row[:, t % 2, :], x_in[t + 2]).then_inc(x_loaded[t % 2], 16)
                for r in range(2):
                    sp.wait_ge(stored[r], 16 * (TILES // 2))

            @block.tensor
            def _(pe):
                for t in range(TILES):
                    last = nc.tensor.transpose(psT[:, t // 4, (t % 4) * P:(t % 4 + 1) * P], H[:, t, :], ident[:])
                last.then_inc(h_turned, 1)
                pe.wait_ge(h_kept, 1)

                def turn(t):
                    pe.wait_ge(added, t + 1)
                    if t >= 2:
                        pe.wait_ge(kept, t - 1)
                    for k in range(KC):
                        last = nc.tensor.transpose(psT[:, t % 2, k * P:(k + 1) * P],
                                                   y_row[:, t % 2, k * P:(k + 1) * P], ident[:])
                    last.then_inc(turned, 1)

                for t in range(TILES):
                    for k in range(KC):
                        nc.tensor.matmul(ps[:, t % 2, :], XT[:, t, k, :], WT[:, k, :], start=k == 0, stop=False)
                    nc.tensor.matmul(ps[:, t % 2, :], HT[:, t, :], BT[:], start=False, stop=True).then_inc(done, 1)
                    if t >= 1:
                        turn(t - 1)
                turn(TILES - 1)

            @block.vector
            def _(dve):
                dve.wait_ge(h_turned, 1)
                nc.vector.tensor_copy(HT[:], psT[:]).then_inc(h_kept, 1)
                for t in range(TILES):
                    dve.wait_ge(done, t + 1)
                    dve.wait_ge(x_loaded[t % 2], 16 * (t // 2 + 1))
                    dve.wait_ge(stored[t % 2], 16 * (t // 2))
                    nc.vector.tensor_tensor(y_row[:, t % 2, :], ps[:, t % 2, :], x_row[:, t % 2, :],
                                            ALU.add).then_inc(added, 1)

            @block.scalar
            def _(act):
                for t in range(TILES):
                    act.wait_ge(turned, t + 1)
                    nc.scalar.copy(XT[:, t, :, :], psT[:, t % 2, :]).then_inc(kept, 1)


def cache_keys(nc, ident, k_cache, kT_pages):
    with Scope(nc) as c:
        PG = P // PSIZE
        n = PAGES // PG
        nat = c.sb("kc_nat", [P, 2, HK * DH])
        out = c.sb("kc_out", [P, 2, PG, HK, PSIZE])
        ps = c.ps("kc_ps", [P, 2, 2, 512])
        loaded = [c.sem(f"kc_loaded{s}") for s in range(2)]
        stored = [c.sem(f"kc_stored{s}") for s in range(2)]
        turned = c.sem("kc_turned")
        kept_dve, kept_act = c.sem("kc_kept_dve"), c.sem("kc_kept_act")
        rows = k_cache.rearrange("(n g) k h d -> n (g k) (h d)", g=PG)
        stores = kT_pages.rearrange("(n g) d m -> n d g m", g=PG)
        block = c.block()

        @block.sync
        def _(sp):
            for s in range(2):
                sp.sem_inc(stored[s], 16)
                sp.dma_start(nat[:, s, :], rows[s]).then_inc(loaded[s], 16)

            def store(m, s):
                sp.wait_ge(kept_dve, m + 3)
                sp.wait_ge(kept_act, m + 3)
                sp.dma_start(stores[m], out[:, s, :, :, :]).then_inc(stored[s], 16)

            with nc.sync.Fori(0, n // 2 - 1) as i:
                for s in range(2):
                    sp.wait_ge(turned, i * 2 + (s + 1))
                    sp.dma_start(nat[:, s, :], rows[i * 2 + (s + 2)]).then_inc(loaded[s], 16)
                    store(i * 2 + s, s)
            for s in range(2):
                store(n - 2 + s, s)
            for s in range(2):
                sp.wait_ge(stored[s], 16 * (n // 2 + 1))

        @block.tensor
        def _(pe):
            with nc.tensor.Fori(0, n // 2) as i:
                for s in range(2):
                    pe.wait_ge(loaded[s], i * 16 + 16)
                    pe.wait_ge(kept_dve, i * 2 + (s + 1))
                    pe.wait_ge(kept_act, i * 2 + (s + 1))
                    for h in range(HK):
                        last = nc.tensor.transpose(ps[:, s, h // 4, (h % 4) * P:(h % 4 + 1) * P],
                                                   nat[:, s, h * DH:(h + 1) * DH], ident[:])
                    last.then_inc(turned, 1)

        def halves(s, half):
            return (out[:, s, :, half * 4:half * 4 + 4, :].rearrange("p g h k -> p h g k"),
                    ps[:, s, half, :].rearrange("p (h g k) -> p h g k", h=4, g=PG))

        @block.vector
        def _(dve):
            dve.sem_inc(kept_dve, 2)
            with nc.vector.Fori(0, n // 2) as i:
                for s in range(2):
                    dve.wait_ge(stored[s], i * 16 + 16)
                    dve.wait_ge(turned, i * 2 + (s + 1))
                    nc.vector.tensor_copy(*halves(s, 0)).then_inc(kept_dve, 1)

        @block.scalar
        def _(act):
            act.sem_inc(kept_act, 2)
            with nc.scalar.Fori(0, n // 2) as i:
                for s in range(2):
                    act.wait_ge(stored[s], i * 16 + 16)
                    act.wait_ge(turned, i * 2 + (s + 1))
                    nc.scalar.copy(*halves(s, 1)).then_inc(kept_act, 1)

def lane_lengths(sp, lens, out, sem):
    by_tile = lens.rearrange("(t j) -> j t", j=BPT)
    for j in range(BPT):
        sp.dma_start(out[j * S:(j + 1) * S, :], by_tile[j:j + 1, :].broadcast_to([S, TILES]),
                     allow_slow_non_contiguous=True).then_inc(sem, 16)


def rope_tables(nc, lens, q_norm_w, k_norm_w, straight, crossed):
    HALF = DH // 2
    inv_freq = (np.float32(1.0) / np.float32(THETA) ** (np.arange(0, DH, 2, dtype=np.float32) / np.float32(DH)))
    TWO_PI_A = 6.28125
    TWO_PI_B = float(np.float32(round((2 * math.pi - TWO_PI_A) * 2 ** 21) / 2 ** 21))
    TWO_PI_C = 2 * math.pi - TWO_PI_A - TWO_PI_B
    ROUND = 1.5 * 2 ** 23
    PI_BELOW = 3.1415925
    with Scope(nc) as c:
        leni, lane = c.sb("rt_leni", [P, TILES], I32), c.sb("rt_lane", [P, 1], I32)
        pos, lanef = c.sb("rt_pos", [P, TILES]), c.sb("rt_lanef", [P, 1])
        inv = c.sb("rt_inv", [P, HALF])
        ang, turns = c.sb("rt_ang", [P, TILES, HALF]), c.sb("rt_turns", [P, TILES, HALF])
        cos, sin = c.sb("rt_cos", [P, TILES, HALF]), c.sb("rt_sin", [P, TILES, HALF])
        w = [c.sb("rt_wq", [P, DH]), c.sb("rt_wk", [P, DH])]
        loaded, lane_made = c.sem("rt_loaded"), c.sem("rt_lane_made")
        chain, reduced, looked_up = c.sem("rt_chain"), c.sem("rt_reduced"), c.sem("rt_looked_up")
        block = c.block()

        @block.sync
        def _(sp):
            lane_lengths(sp, lens, leni, loaded)
            for x, src in zip(w, (q_norm_w, k_norm_w)):
                sp.dma_start(x[:], src.rearrange("(a d) -> a d", a=1).broadcast_to([P, DH])).then_inc(loaded, 16)

        @block.gpsimd
        def _(pool):
            for j in range(BPT):
                nc.gpsimd.iota(lane[j * S:(j + 1) * S, :], pattern=[[0, 1]], base=0,
                               channel_multiplier=1).then_inc(lane_made, 1)
                pool.wait_ge(lane_made, j + 1)

        @block.vector
        def _(dve):
            steps = [0]

            def link(ins):
                steps[0] += 1
                ins.then_inc(chain, 1)
                dve.wait_ge(chain, steps[0])

            for i in range(HALF):
                nc.vector.memset(inv[:, i:i + 1], float(inv_freq[i]))
            dve.wait_ge(lane_made, BPT)
            dve.wait_ge(loaded, 16 * (BPT + 2))
            nc.vector.tensor_copy(lanef[:], lane[:])
            link(nc.vector.tensor_copy(pos[:], leni[:]))
            link(nc.vector.tensor_scalar(pos[:], pos[:], lanef[:, 0:1], None, ALU.add))
            link(nc.vector.tensor_tensor(ang[:], pos[:].unsqueeze(2).broadcast_to([P, TILES, HALF]),
                                         inv[:].unsqueeze(1).broadcast_to([P, TILES, HALF]), ALU.mult))
            link(nc.vector.tensor_scalar(turns[:], ang[:], 1.0 / (2 * math.pi), None, ALU.mult))
            link(nc.vector.tensor_scalar(turns[:], turns[:], ROUND, None, ALU.add))
            link(nc.vector.tensor_scalar(turns[:], turns[:], -ROUND, None, ALU.add))
            for part in (TWO_PI_A, TWO_PI_B, TWO_PI_C):
                link(nc.vector.scalar_tensor_tensor(out=ang[:], in0=turns[:], scalar=-part, in1=ang[:],
                                                    op0=ALU.mult, op1=ALU.add))
            link(nc.vector.tensor_scalar(ang[:], ang[:], PI_BELOW, -PI_BELOW, ALU.min, ALU.max))
            link(nc.vector.tensor_scalar(turns[:], ang[:], -1.0, None, ALU.mult))
            link(nc.vector.tensor_tensor(turns[:], turns[:], ang[:], ALU.min))
            nc.vector.tensor_scalar(turns[:], turns[:], math.pi / 2, None, ALU.add).then_inc(reduced, 1)
            dve.wait_ge(looked_up, 2)
            for kind in range(2):
                for out, table, order in ((straight, cos, (0, 1)), (crossed, sin, (1, 0))):
                    for half in range(2):
                        wh = w[kind][:, order[half] * HALF:(order[half] + 1) * HALF]
                        sign = -1.0 if out is crossed and half == 0 else 1.0
                        nc.vector.scalar_tensor_tensor(out=out[:, kind, :, half, :], in0=table[:], scalar=sign,
                                                       in1=wh.unsqueeze(1).broadcast_to([P, TILES, HALF]),
                                                       op0=ALU.mult, op1=ALU.mult)

        @block.scalar
        def _(act):
            act.wait_ge(reduced, 1)
            nc.scalar.activation(sin[:], ang[:], ACT.Sin).then_inc(looked_up, 1)
            nc.scalar.activation(cos[:], turns[:], ACT.Sin).then_inc(looked_up, 1)


def split(nc, XT, XH, XL):
    with Scope(nc) as c:
        high = c.sem("sp_high")
        block = c.block()

        @block.scalar
        def _(act):
            for t in range(0, TILES, 4):
                nc.scalar.copy(XH[:, t:t + 4, :, :], XT[:, t:t + 4, :, :]).then_inc(high, 1)

        @block.vector
        def _(dve):
            for t in range(0, TILES, 4):
                dve.wait_ge(high, t // 4 + 1)
                nc.vector.tensor_tensor(XL[:, t:t + 4, :, :], XT[:, t:t + 4, :, :],
                                        XH[:, t:t + 4, :, :].bitcast(F32), ALU.subtract)


def project(nc, ident, XH, XL, straight, crossed, Wq, Wk, Wv, qT, kT_own, v_own):
    CQ, CK = HQ // 4, HK // 4
    CHUNKS = CQ + 2 * CK
    FIRST_K, FIRST_V = CQ, CQ + CK
    LOOPED = CQ - 2
    HALF = DH // 2

    def kind(chunk):
        if not isinstance(chunk, int) or chunk < FIRST_K:
            return 0
        return 1 if chunk < FIRST_V else 2

    def chunks(eng, body):
        with eng.Fori(0, LOOPED // 2) as i:
            for s in range(2):
                body(i * 2 + s, s)
        for chunk in range(LOOPED, CHUNKS):
            body(chunk, chunk % 2)

    def known(chunk):
        return isinstance(chunk, int)

    by_rows = [w.rearrange("(c o p) k -> c p o k", p=P, o=KC) for w in (Wq, Wk, Wv)]

    def rows_of(chunk):
        return by_rows[kind(chunk)][chunk - (0, FIRST_K, FIRST_V)[kind(chunk)] if known(chunk) else chunk]

    with Scope(nc) as c:
        nat = c.sb("pr_nat", [P, 2, KC, D])
        WH, WL = c.sb("pr_WH", [P, 2, KC, D], F32R), c.sb("pr_WL", [P, 2, KC, D], F32R)
        junk = c.sb("pr_junk", [P, 4, DH])
        eps = c.sb("pr_eps", [P, 1])
        sums, root, rstd = (c.sb(f"pr_{x}", [P, 2, 4]) for x in ("sums", "root", "rstd"))
        u, m1, m2, y = (c.sb(f"pr_{x}", [P, 2, 4, 2, HALF]) for x in ("u", "m1", "m2", "y"))
        turned_out = c.sb("pr_turned_out", [P, 2, BPT, 4, S])
        v_out = c.sb("pr_v_out", [P, 2, D])
        psW = c.ps("pr_psW", [P, KC, D])
        ps, psT = c.ps("pr_ps", [P, 2, D]), c.ps("pr_psT", [P, 2, D])
        w_loaded = [c.sem(f"pr_w_loaded{s}") for s in range(2)]
        w_turned, w_high, w_low = c.sem("pr_w_turned"), c.sem("pr_w_high"), c.sem("pr_w_low")
        eps_made = c.sem("pr_eps_made")
        done = c.sem("pr_done")
        squared, rooted, scaled = c.sem("pr_squared"), c.sem("pr_rooted"), c.sem("pr_scaled")
        inverted = c.sem("pr_inverted")
        straight_done, crossed_done, summed = c.sem("pr_straight"), c.sem("pr_crossed"), c.sem("pr_summed")
        turned, kept = c.sem("pr_turned"), c.sem("pr_kept")
        v_kept = c.sem("pr_v_kept")
        stored = [c.sem(f"pr_stored{s}") for s in range(2)]
        v_stored = [c.sem(f"pr_v_stored{s}") for s in range(2)]
        block = c.block()

        @block.sync
        def _(sp):
            for s in range(2):
                sp.sem_inc(stored[s], 16)
                sp.dma_start(nat[:, s, :, :], rows_of(s)).then_inc(w_loaded[s], 16)

            def body(chunk, s):
                if not known(chunk) or chunk + 2 < CHUNKS:
                    sp.wait_ge(w_turned, chunk + 1)
                    sp.dma_start(nat[:, s, :, :], rows_of(chunk + 2)).then_inc(w_loaded[s], 16)
                for t in range(TILES):
                    r = t % 2
                    if kind(chunk) == 2:
                        sp.wait_ge(v_kept, (chunk - FIRST_V) * TILES + t + 1)
                        sp.dma_start(v_own[t, :, chunk - FIRST_V, :], v_out[:, r, :]).then_inc(v_stored[r], 16)
                        continue
                    sp.wait_ge(kept, chunk * TILES + (t + 3))
                    store = (qT[t * BPT:(t + 1) * BPT, :, chunk, :] if kind(chunk) == 0
                             else kT_own[t * BPT:(t + 1) * BPT, :, chunk - FIRST_K, :])
                    sp.dma_start(store.rearrange("j d m -> d j m"),
                                 turned_out[:, r, :, :, :].rearrange("d j g s -> d j (g s)")).then_inc(stored[r], 16)

            chunks(nc.sync, body)
            for r in range(2):
                sp.wait_ge(stored[r], 16 * (FIRST_V * TILES // 2 + 1))
                sp.wait_ge(v_stored[r], 16 * (CK * TILES // 2))

        @block.tensor
        def _(pe):
            pe.sem_inc(turned, 2)

            def turn_weights(chunk, s):
                pe.wait_ge(w_loaded[s], (chunk // 2) * 16 + 16 if known(chunk) else (chunk - s) * 8 + 16)
                pe.wait_ge(w_low, chunk)
                for k in range(KC):
                    for o in range(KC):
                        last = nc.tensor.transpose(psW[:, k, o * P:(o + 1) * P], nat[:, s, o, k * P:(k + 1) * P],
                                                   ident[:])
                last.then_inc(w_turned, 1)

            def products(chunk, s, t):
                unit = chunk * TILES + t
                if t == 0:
                    pe.wait_ge(w_low, chunk + 1)
                if known(chunk) and unit - 2 >= FIRST_V * TILES:
                    pe.wait_ge(v_kept, unit - 1 - FIRST_V * TILES)
                elif not known(chunk) or unit >= 2:
                    pe.wait_ge(scaled, unit - 1)
                for k in range(KC):
                    for n, (x, w) in enumerate(((XH, WH), (XH, WL), (XL, WH))):
                        last = nc.tensor.matmul(ps[:, t % 2, :], x[:, t, k, :], w[:, s, k, :],
                                                start=k == 0 and n == 0, stop=k == KC - 1 and n == 2)
                last.then_inc(done, 1)

            def turn(chunk, t):
                unit = chunk * TILES + t
                pe.wait_ge(summed, unit + 1)
                pe.wait_ge(kept, unit + 1)
                for g in range(4):
                    last = nc.tensor.transpose(psT[:, t % 2, g * P:(g + 1) * P],
                                               y[:, t % 2, g, :, :].rearrange("p a b -> p (a b)"), ident[:])
                last.then_inc(turned, 1)

            def body(chunk, s):
                for t in range(TILES):
                    if t + 2 < TILES:
                        products(chunk, s, t + 2)
                    elif not known(chunk) or chunk + 1 < CHUNKS:
                        products(chunk + 1, 1 - s, t + 2 - TILES)
                    if kind(chunk) < 2:
                        turn(chunk, t)
                if not known(chunk) or chunk + 2 < CHUNKS:
                    turn_weights(chunk + 2, s)

            turn_weights(0, 0)
            turn_weights(1, 1)
            for t in range(2):
                products(0, 0, t)
            chunks(nc.tensor, body)

        @block.scalar
        def _(act):
            act.sem_inc(kept, 2)
            act.wait_ge(eps_made, 1)

            def high(chunk, s):
                act.wait_ge(w_turned, chunk + 1)
                nc.scalar.copy(WH[:, s, :, :], psW[:]).then_inc(w_high, 1)

            def front(chunk, t):
                unit, r = chunk * TILES + t, t % 2
                act.wait_ge(done, unit + 1)
                if kind(chunk) == 2:
                    act.wait_ge(v_stored[r], 16 * ((unit - FIRST_V * TILES) // 2))
                    nc.scalar.copy(v_out[:, r, :], ps[:, r, :]).then_inc(v_kept, 1)
                    return
                for g in range(4):
                    nc.scalar.activation(junk[:, g, :], ps[:, r, g * DH:(g + 1) * DH], ACT.Square,
                                         accum_out=sums[:, r, g:g + 1]).then_inc(squared, 1)
                act.wait_ge(squared, unit * 4 + 4)
                nc.scalar.activation(root[:, r, :], sums[:, r, :], ACT.Sqrt, bias=eps[:],
                                     scale=1.0 / DH).then_inc(rooted, 1)

            def back(chunk, t):
                unit, r = chunk * TILES + t, t % 2
                act.wait_ge(turned, unit + 3)
                act.wait_ge(stored[r], (chunk * (TILES // 2) + (t // 2 + 1)) * 16)
                nc.scalar.copy(turned_out[:, r, :, :, :].rearrange("p j g s -> p g j s"),
                               psT[:, r, :].rearrange("p (g j s) -> p g j s", g=4, j=BPT)).then_inc(kept, 1)

            def body(chunk, s):
                for t in range(TILES):
                    if t + 2 < TILES:
                        front(chunk, t + 2)
                    elif not known(chunk) or chunk + 1 < CHUNKS:
                        front(chunk + 1, t + 2 - TILES)
                    if kind(chunk) < 2:
                        back(chunk, t)
                if not known(chunk) or chunk + 2 < CHUNKS:
                    high(chunk + 2, s)

            high(0, 0)
            high(1, 1)
            for t in range(2):
                front(0, t)
            chunks(nc.scalar, body)

        @block.vector
        def _(dve):
            nc.vector.memset(eps[:], EPS).then_inc(eps_made, 1)

            def low(chunk, s):
                dve.wait_ge(w_high, chunk + 1)
                nc.vector.tensor_tensor(WL[:, s, :, :], psW[:], WH[:, s, :, :].bitcast(F32),
                                        ALU.subtract).then_inc(w_low, 1)

            def rope(chunk, t):
                unit, r, kd = chunk * TILES + t, t % 2, kind(chunk)
                dve.wait_ge(rooted, unit + 1)
                nc.vector.reciprocal(rstd[:, r, :], root[:, r, :]).then_inc(inverted, 1)
                dve.wait_ge(inverted, unit + 1)
                nc.vector.tensor_tensor(u[:, r, :, :, :].rearrange("p g a b -> p g (a b)"),
                                        ps[:, r, :].rearrange("p (g d) -> p g d", g=4),
                                        rstd[:, r, :].unsqueeze(2).broadcast_to([P, 4, DH]),
                                        ALU.mult).then_inc(scaled, 1)
                dve.wait_ge(scaled, unit + 1)
                table = straight[:, kd, t, :, :].rearrange("p a b -> p (a b)").unsqueeze(1)
                nc.vector.tensor_tensor(m1[:, r, :, :, :].rearrange("p g a b -> p g (a b)"),
                                        u[:, r, :, :, :].rearrange("p g a b -> p g (a b)"),
                                        table.broadcast_to([P, 4, DH]), ALU.mult).then_inc(straight_done, 1)
                dve.wait_ge(straight_done, unit + 1)
                dve.wait_ge(crossed_done, unit + 1)
                dve.wait_ge(turned, unit + 1)
                nc.vector.tensor_tensor(y[:, r, :, :, :], m1[:, r, :, :, :], m2[:, r, :, :, :],
                                        ALU.add).then_inc(summed, 1)

            def body(chunk, s):
                if kind(chunk) < 2:
                    for t in range(TILES):
                        rope(chunk, t)
                if not known(chunk) or chunk + 2 < CHUNKS:
                    low(chunk + 2, s)

            low(0, 0)
            low(1, 1)
            chunks(nc.vector, body)

        @block.gpsimd
        def _(pool):
            def cross(chunk, t):
                unit, r, kd = chunk * TILES + t, t % 2, kind(chunk)
                pool.wait_ge(scaled, unit + 1)
                for half in range(2):
                    table = crossed[:, kd, t, half, :].unsqueeze(1).broadcast_to([P, 4, HALF])
                    last = nc.gpsimd.tensor_tensor(m2[:, r, :, half, :], u[:, r, :, 1 - half, :], table, ALU.mult)
                last.then_inc(crossed_done, 1)

            def body(chunk, s):
                if kind(chunk) < 2:
                    for t in range(TILES):
                        cross(chunk, t)

            chunks(nc.gpsimd, body)


def attention(nc, ident, table, lens, qT, kT_pages, kT_own, v_cache, v_own, oT):
    UNITS = B * HK
    KEYS = L + S
    CH = L // P
    with Scope(nc) as c:
        K = c.sb("at_K", [P, 2, NPP + 1, HK, PSIZE])
        V = c.sb("at_V", [P, 2, CH + 1, HK * DH])
        Q = c.sb("at_Q", [P, 2, HK, P])
        out = c.sb("at_out", [P, 2, HK, P])
        tab = c.sb("at_tab", [1, B * NPP], I32)
        tab_all = c.sb("at_tab_all", [P, B * CH, BPT], I32)
        lane, rows = c.sb("at_lane", [P, 1], I32), c.sb("at_rows", [P, B * CH], I32)
        lanef, rowsf = c.sb("at_lanef", [P, 1]), c.sb("at_rowsf", [P, B * CH])
        rows_slot = c.sb("at_rows_slot", [P, 2, CH], I32)
        lensi, lensf = c.sb("at_lensi", [P, B], I32), c.sb("at_lensf", [P, B])
        keyi, keyf = c.sb("at_keyi", [P, L], I32), c.sb("at_keyf", [P, L])
        mask = c.sb("at_mask", [P, 2, KEYS])
        scores, probs = c.sb("at_scores", [P, 2, KEYS]), c.sb("at_probs", [P, 2, KEYS])
        least = c.sb("at_least", [P, 2])
        total, inverse = c.sb("at_total", [P, 4]), c.sb("at_inverse", [P, 2])
        PT = c.sb("at_PT", [P, 2, CH + 1, P])
        O = c.sb("at_O", [P, 2, DH])
        psS = c.ps("at_psS", [P, 2, 1024])
        psP, psX, psO = c.ps("at_psP", [P, CH, P]), c.ps("at_psX", [P, 512]), c.ps("at_psO", [P, 512])

        table_loaded, lens_loaded = c.sem("at_table_loaded"), c.sem("at_lens_loaded")
        counted, prepared = c.sem("at_counted"), c.sem("at_prepared")
        k_loaded = [c.sem(f"at_k_loaded{s}") for s in range(2)]
        v_loaded = [c.sem(f"at_v_loaded{s}") for s in range(2)]
        v_own_loaded = [c.sem(f"at_v_own_loaded{s}") for s in range(2)]
        stored = [c.sem(f"at_stored{s}") for s in range(2)]
        rows_copied, rows_seen = c.sem("at_rows_copied"), c.sem("at_rows_seen")
        scored = c.sem("at_scored")
        masked = c.sem("at_masked")
        mask_made = c.sem("at_mask_made")
        exped = c.sem("at_exped")
        turned = c.sem("at_turned")
        cached_kept, own_kept = c.sem("at_cached_kept"), c.sem("at_own_kept")
        weighted = c.sem("at_weighted")
        inverted, divided = c.sem("at_inverted"), c.sem("at_divided")
        out_kept = c.sem("at_out_kept")
        block = c.block()

        def known(b):
            return isinstance(b, int)

        def batches(eng, body):
            for b in range(2):
                body(b, b)
            with eng.Fori(1, B // 2 - 1) as i:
                for s in range(2):
                    body(i * 2 + s, s)
            for b in range(B - 2, B):
                body(b, b % 2)

        def exists(b, h):
            return not known(b) or 0 <= b * HK + h < UNITS

        def at(b, s, h):
            return b + h // HK, (s + h // HK) % 2, h % HK

        def wait_loads(eng, sem, b, s, n):
            eng.wait_ge(sem, (b // 2 + 1) * (16 * n) if known(b) else (b - s) * (8 * n) + 16 * n)

        @block.sync
        def _(sp):
            lens_row = lens.rearrange("(a b) -> a b", a=1)
            table_row = table.rearrange("(a b) n -> a (b n)", a=1)
            sp.dma_start(tab[:], table_row).then_inc(table_loaded, 16)
            sp.dma_start(tab_all[:].rearrange("p c j -> p (c j)"),
                         table_row.broadcast_to([P, B * NPP])).then_inc(table_loaded, 16)
            sp.dma_start(lensi[:], lens_row.broadcast_to([P, B])).then_inc(lens_loaded, 16)
            sp.wait_ge(table_loaded, 32)

            def load_keys(b, s):
                sp.dma_start(Q[:, s, :, :], qT[b]).then_inc(k_loaded[s], 16)
                sp.dma_start(K[:, s, NPP, :, :].rearrange("d h k -> d (h k)").rearrange("d (c m) -> d c m", c=2),
                             kT_own[b]).then_inc(k_loaded[s], 16)
                for n in range(NPP):
                    page = nc.sync.value_load(tab[0:1, ds(b * NPP + n, 1)], min_val=0, max_val=PAGES - 1)
                    sp.dma_start(K[:, s, n, :, :].rearrange("d h k -> d (h k)"),
                                 kT_pages[page]).then_inc(k_loaded[s], 16)

            def load_own_values(b, s):
                sp.dma_start(V[0:S, s, CH, :], v_own[b]).then_inc(v_own_loaded[s], 16)

            for b in range(2):
                load_keys(b, b)
                load_own_values(b, b)

            def body(b, s):
                if not known(b) or b + 2 < B:
                    sp.wait_ge(scored, b * HK + HK)
                    load_keys(b + 2, s)
                    sp.wait_ge(weighted, b * HK + HK)
                    load_own_values(b + 2, s)
                sp.wait_ge(out_kept, b * HK + HK)
                sp.dma_start(oT[b], out[:, s, :, :].rearrange("d h m -> d (h m)")).then_inc(stored[s], 16)

            batches(nc.sync, body)
            for s in range(2):
                sp.wait_ge(stored[s], 16 * (B // 2))

        @block.gpsimd
        def _(pool):
            nc.gpsimd.iota(keyi[:], pattern=[[1, L]], base=0, channel_multiplier=0).then_inc(counted, 1)
            for j in range(BPT):
                pool.wait_ge(counted, j + 1)
                nc.gpsimd.iota(lane[j * S:(j + 1) * S, :], pattern=[[0, 1]], base=0,
                               channel_multiplier=1).then_inc(counted, 1)
            pool.wait_ge(prepared, 1)
            v_rows = v_cache.rearrange("a k h d -> (a k) (h d)")

            def load_values(b, s):
                nc.gpsimd.tensor_copy(rows_slot[:, s, :], rows[:, ds(b * CH, CH)]).then_inc(rows_copied, 1)
                pool.wait_ge(rows_copied, b + 1)
                pool.sem_inc(rows_seen, 1)
                for n in range(CH):
                    pool.indirect_dma_start(
                        out=V[:, s, n, :], out_offset=None, in_=v_rows,
                        in_offset=bass.IndirectOffsetOnAxis(ap=rows_slot[:, s, n:n + 1], axis=0),
                    ).then_inc(v_loaded[s], 16)

            for b in range(2):
                load_values(b, b)

            def body(b, s):
                if not known(b) or b + 2 < B:
                    pool.wait_ge(weighted, b * HK + HK)
                    wait_loads(pool, v_loaded[s], b, s, CH)
                    load_values(b + 2, s)

            batches(nc.gpsimd, body)

        @block.tensor
        def _(pe):
            def score(b, s, h):
                unit = b * HK + h
                if h == 0:
                    wait_loads(pe, k_loaded[s], b, s, NPP + 2)
                if not known(b) or unit >= 2:
                    pe.wait_ge(masked, unit - 1)
                nc.tensor.matmul(psS[:, h % 2, 0:L].rearrange("p (n k) -> p n k", n=NPP), Q[:, s, h, :],
                                 K[:, s, 0:NPP, h, :], start=True, stop=True)
                nc.tensor.matmul(psS[:, h % 2, L:KEYS], Q[:, s, h, :], K[:, s, NPP, h, :],
                                 start=True, stop=True).then_inc(scored, 1)

            def turn(b, h, result):
                unit = b * HK + h
                if exists(b, h):
                    pe.wait_ge(exped, unit + 1)
                if exists(b, h - 1):
                    pe.wait_ge(cached_kept, unit if exists(b, h) else UNITS)
                    pe.wait_ge(own_kept, unit if exists(b, h) else UNITS)
                if exists(b, h - 3):
                    pe.wait_ge(out_kept, unit - 2)
                if exists(b, h):
                    for n in range(CH):
                        last = nc.tensor.transpose(psP[:, n, :], probs[:, h % 2, n * P:(n + 1) * P], ident[:])
                    last = nc.tensor.transpose(psX[0:S, 0:P], probs[:, h % 2, L:KEYS], ident[:])
                if result:
                    pe.wait_ge(divided, unit - 1)
                    last = nc.tensor.transpose(psX[:, P:2 * P], O[:, h % 2, :], ident[:])
                last.then_inc(turned, 1)

            def weigh(b, s, h):
                unit = b * HK + h
                if h == 0:
                    wait_loads(pe, v_loaded[s], b, s, CH)
                    wait_loads(pe, v_own_loaded[s], b, s, 1)
                pe.wait_ge(cached_kept, unit + 1)
                pe.wait_ge(own_kept, unit + 1)
                pe.wait_ge(divided, unit)
                for n in range(CH):
                    nc.tensor.matmul(psO[:, 0:DH], PT[:, h % 2, n, :], V[:, s, n, h * DH:(h + 1) * DH],
                                     start=n == 0, stop=False)
                nc.tensor.matmul(psO[:, 0:DH], PT[0:S, h % 2, CH, :], V[0:S, s, CH, h * DH:(h + 1) * DH],
                                 start=False, stop=True).then_inc(weighted, 1)

            score(0, 0, 0)
            score(0, 0, 1)
            turn(0, 0, False)

            def body(b, s):
                for h in range(HK):
                    if exists(b, h + 2):
                        score(*at(b, s, h + 2))
                    turn(b, h + 1, exists(b, h - 1))
                    weigh(b, s, h)

            batches(nc.tensor, body)
            turn(B - 1, HK + 1, True)

        @block.vector
        def _(dve):
            dve.wait_ge(lens_loaded, 16)
            dve.wait_ge(table_loaded, 32)
            dve.wait_ge(counted, 1 + BPT)
            nc.vector.tensor_copy(lensf[:], lensi[:])
            nc.vector.tensor_copy(keyf[:], keyi[:])
            nc.vector.tensor_copy(lanef[:], lane[:])
            for j in range(BPT):
                nc.vector.tensor_copy(rowsf[j * S:(j + 1) * S, :], tab_all[j * S:(j + 1) * S, :, j])
            nc.vector.memset(mask[:], 0.0).then_inc(inverted, 1)
            dve.wait_ge(inverted, 1)
            nc.vector.tensor_scalar(rows[:], rowsf[:], float(PSIZE), lanef[:, 0:1], ALU.mult,
                                    ALU.add).then_inc(prepared, 1)

            def invert(unit, h):
                dve.wait_ge(exped, unit - 1)
                nc.vector.reciprocal(inverse[:, h % 2:h % 2 + 1],
                                     total[:, (h + 2) % 4:(h + 2) % 4 + 1]).then_inc(inverted, 1)

            def mask_scores(b, s, h):
                unit = b * HK + h
                if h == 0:
                    nc.vector.tensor_scalar(mask[:, s, 0:L], keyf[:], lensf[:, ds(b, 1)], MASKED, ALU.is_ge,
                                            ALU.mult).then_inc(mask_made, 1)
                    dve.wait_ge(mask_made, b + 1)
                dve.wait_ge(scored, unit + 1)
                if not known(b) or unit >= 2:
                    invert(unit, h)
                nc.vector.tensor_tensor_reduce(out=scores[:, h % 2, :], in0=psS[:, h % 2, 0:KEYS],
                                               in1=mask[:, s, :], scale=-SCALE, scalar=-MASKED, op0=ALU.add,
                                               op1=ALU.min, accum_out=least[:, h % 2:h % 2 + 1]).then_inc(masked, 1)

            def keep_own(b, h):
                unit = b * HK + h
                dve.wait_ge(turned, unit + 1)
                if not known(b) or unit >= 2:
                    dve.wait_ge(weighted, unit - 1)
                nc.vector.tensor_copy(PT[0:S, h % 2, CH, :], psX[0:S, 0:P]).then_inc(own_kept, 1)

            def keep_out(b, s, h):
                b, s, h = at(b, s, h)
                dve.wait_ge(turned, b * HK + h + 3)
                if h == 0:
                    dve.wait_ge(stored[s], (b // 2) * 16 if known(b) else (b - s) * 8)
                nc.vector.tensor_copy(out[:, s, h, :], psX[:, P:2 * P]).then_inc(out_kept, 1)

            def divide(b, h):
                unit = b * HK + h
                dve.wait_ge(inverted, unit + 2)
                dve.wait_ge(weighted, unit + 1)
                if not known(b) or unit >= 2:
                    dve.wait_ge(turned, unit)
                nc.vector.tensor_scalar(O[:, h % 2, :], psO[:, 0:DH], inverse[:, h % 2:h % 2 + 1], None,
                                        ALU.mult).then_inc(divided, 1)

            mask_scores(0, 0, 0)
            mask_scores(0, 0, 1)
            keep_own(0, 0)

            def body(b, s):
                for h in range(HK):
                    if exists(b, h + 2):
                        mask_scores(*at(b, s, h + 2))
                    else:
                        invert(b * HK + h + 2, h + 2)
                    if exists(b, h + 1):
                        keep_own(b, h + 1)
                    if exists(b, h - 1):
                        keep_out(b, s, h - 1)
                    divide(b, h)

            batches(nc.vector, body)
            keep_out(B - 1, (B - 1) % 2, HK - 1)

        @block.scalar
        def _(act):
            def exp(b, h):
                unit = b * HK + h
                act.wait_ge(masked, unit + 1)
                if not known(b) or unit >= 2:
                    act.wait_ge(turned, unit - 1)
                if not known(b) or unit >= 4:
                    act.wait_ge(inverted, unit - 2)
                nc.scalar.activation(probs[:, h % 2, :], scores[:, h % 2, :], ACT.Exp,
                                     bias=least[:, h % 2:h % 2 + 1], scale=-1.0,
                                     accum_out=total[:, h % 4:h % 4 + 1]).then_inc(exped, 1)

            def keep_cached(b, h):
                unit = b * HK + h
                act.wait_ge(turned, unit + 1)
                if not known(b) or unit >= 2:
                    act.wait_ge(weighted, unit - 1)
                nc.scalar.copy(PT[:, h % 2, 0:CH, :], psP[:]).then_inc(cached_kept, 1)

            exp(0, 0)
            exp(0, 1)
            keep_cached(0, 0)

            def body(b, s):
                for h in range(HK):
                    if exists(b, h + 1):
                        keep_cached(b, h + 1)
                    if exists(b, h + 2):
                        exp(b, h + 2)

            batches(nc.scalar, body)


def output_layer(nc, ident, Wo, oT, x_in, result):
    HALF = HQ // 2
    BLOCKS = HQ * DH // D
    with Scope(nc) as c:
        WH, WL = c.sb("ol_WH", [P, HQ, D], F32R), c.sb("ol_WL", [P, HQ, D], F32R)

        with Scope(nc) as w:
            nat = w.sb("ol_nat", [P, 2, KC, D])
            ps = w.ps("ol_psW", [P, 2, KC, D])
            loaded = [w.sem(f"ol_w_loaded{s}") for s in range(2)]
            turned, high, low = w.sem("ol_w_turned"), w.sem("ol_w_high"), w.sem("ol_w_low")
            blocks = Wo.rearrange("(o p) (a k) -> a p o k", p=P, k=D)
            block = w.block()

            @block.sync
            def _(sp):
                for a in range(BLOCKS):
                    if a >= 2:
                        sp.wait_ge(turned, a - 1)
                    sp.dma_start(nat[:, a % 2, :, :], blocks[a]).then_inc(loaded[a % 2], 16)

            @block.tensor
            def _(pe):
                pe.sem_inc(low, 2)
                with nc.tensor.Fori(0, BLOCKS // 2) as i:
                    for s in range(2):
                        pe.wait_ge(loaded[s], i * 16 + 16)
                        pe.wait_ge(low, i * 2 + (s + 1))
                        for k in range(KC):
                            for o in range(KC):
                                last = nc.tensor.transpose(ps[:, s, k, o * P:(o + 1) * P],
                                                           nat[:, s, o, k * P:(k + 1) * P], ident[:])
                        last.then_inc(turned, 1)

            @block.scalar
            def _(act):
                with nc.scalar.Fori(0, BLOCKS // 2) as i:
                    for s in range(2):
                        act.wait_ge(turned, i * 2 + (s + 1))
                        nc.scalar.copy(WH[:, ds(i * (2 * KC) + s * KC, KC), :], ps[:, s, :, :]).then_inc(high, 1)

            @block.vector
            def _(dve):
                with nc.vector.Fori(0, BLOCKS // 2) as i:
                    for s in range(2):
                        heads = ds(i * (2 * KC) + s * KC, KC)
                        dve.wait_ge(high, i * 2 + (s + 1))
                        nc.vector.tensor_tensor(WL[:, heads, :], ps[:, s, :, :], WH[:, heads, :].bitcast(F32),
                                                ALU.subtract).then_inc(low, 1)

        with Scope(nc) as w:
            o = w.sb("ol_o", [P, 2, BPT, HALF, S])
            OH, OL = w.sb("ol_OH", [P, 2, HALF, P], F32R), w.sb("ol_OL", [P, 2, HALF, P], F32R)
            x_row, y_row = w.sb("ol_x_row", [P, 2, D]), w.sb("ol_y_row", [P, 2, D])
            ps = w.ps("ol_ps", [P, 2, D])
            loaded = [w.sem(f"ol_loaded{s}") for s in range(2)]
            x_loaded = [w.sem(f"ol_x_loaded{s}") for s in range(2)]
            stored = [w.sem(f"ol_stored{s}") for s in range(2)]
            high, low, done, added = (w.sem(f"ol_{x}") for x in ("high", "low", "done", "added"))
            block = w.block()

            @block.sync
            def _(sp):
                def load(t, half):
                    sp.dma_start(o[:, half, :, :, :].rearrange("d j h s -> d j (h s)"),
                                 oT[ds(t * BPT, BPT), :, half * HALF * S:(half + 1) * HALF * S]
                                 .rearrange("j d m -> d j m")).then_inc(loaded[half], 16)

                def load_x(t, r):
                    sp.dma_start(x_row[:, r, :], x_in[t]).then_inc(x_loaded[r], 16)

                def store(t, r):
                    sp.wait_ge(added, t + 1)
                    sp.dma_start(result[t], y_row[:, r, :]).then_inc(stored[r], 16)

                for r in range(2):
                    sp.sem_inc(stored[r], 16)
                load(0, 0)
                load(0, 1)
                load_x(0, 0)
                load_x(1, 1)
                with nc.sync.Fori(0, TILES // 2 - 1) as i:
                    for r in range(2):
                        t = i * 2 + r
                        for half in range(2):
                            sp.wait_ge(low, t * 2 + (half + 1))
                            load(t + 1, half)
                        store(t, r)
                        load_x(t + 2, r)
                for half in range(2):
                    sp.wait_ge(low, TILES * 2 - 3 + half)
                    load(TILES - 1, half)
                for r in range(2):
                    store(TILES - 2 + r, r)
                for r in range(2):
                    sp.wait_ge(stored[r], 16 * (TILES // 2 + 1))

            @block.scalar
            def _(act):
                act.sem_inc(done, 2)
                with nc.scalar.Fori(0, TILES) as t:
                    for half in range(2):
                        act.wait_ge(loaded[half], t * 16 + 16)
                        act.wait_ge(done, t * 2 + (half + 1))
                        nc.scalar.copy(OH[:, half, :, :].rearrange("d h (j s) -> d j h s", j=BPT),
                                       o[:, half, :, :, :]).then_inc(high, 1)

            @block.vector
            def _(dve):
                def low_parts(t):
                    for half in range(2):
                        dve.wait_ge(high, t * 2 + (half + 1))
                        dve.wait_ge(done, t * 2 + (half + 1))
                        nc.vector.tensor_tensor(
                            OL[:, half, :, :].rearrange("d h (j s) -> d j h s", j=BPT), o[:, half, :, :, :],
                            OH[:, half, :, :].bitcast(F32).rearrange("d h (j s) -> d j h s", j=BPT),
                            ALU.subtract).then_inc(low, 1)

                def add(t, i, r):
                    dve.wait_ge(done, t * 2 + 4)
                    dve.wait_ge(x_loaded[r], i * 16 + 16)
                    dve.wait_ge(stored[r], i * 16 + 16)
                    nc.vector.tensor_tensor(y_row[:, r, :], ps[:, r, :], x_row[:, r, :],
                                            ALU.add).then_inc(added, 1)

                low_parts(0)
                with nc.vector.Fori(0, TILES // 2 - 1) as i:
                    for r in range(2):
                        low_parts(i * 2 + (r + 1))
                        add(i * 2 + r, i, r)
                low_parts(TILES - 1)
                for r in range(2):
                    add(TILES - 2 + r, TILES // 2 - 1, r)

            @block.tensor
            def _(pe):
                def products(t, r, first):
                    if not first:
                        pe.wait_ge(added, t - 1)
                    for half in range(2):
                        pe.wait_ge(low, t * 2 + (half + 1))
                        for h in range(HALF):
                            for n, (x, wt) in enumerate(((OH, WH), (OH, WL), (OL, WH))):
                                last = nc.tensor.matmul(ps[:, r, :], x[:, half, h, :], wt[:, half * HALF + h, :],
                                                        start=half == 0 and h == 0 and n == 0,
                                                        stop=half == 1 and h == HALF - 1 and n == 2)
                        last.then_inc(done, 1)

                products(0, 0, True)
                products(1, 1, True)
                with nc.tensor.Fori(1, TILES // 2) as i:
                    for r in range(2):
                        products(i * 2 + r, r, False)


def build(nc, x, ids0, ids1, ids2, table, lens, w0, W, Wr, A, Bm, w2, Wq, Wk, Wv, Wo, q_norm_w, k_norm_w,
          k_cache, v_cache, out):
    def dram(name, shape):
        return nc.dram_tensor(name, shape, F32, kind="Internal").ap()

    x_tiles = x.rearrange("(t j) s d -> t (j s) d", j=BPT)
    out_tiles = out.rearrange("(t j) s d -> t (j s) d", j=BPT)
    x1, x2, x3 = (dram(f"x{n}", [TILES, P, D]) for n in (1, 2, 3))
    qT = dram("qT", [B, DH, HK, P])
    kT_own = dram("kT_own", [B, DH, 2, P])
    v_own = dram("v_own", [TILES, P, 2, D])
    kT_pages = dram("kT_pages", [PAGES, DH, HK * PSIZE])
    oT = dram("oT", [B, DH, HQ * S])

    with Scope(nc) as whole:
        ident = whole.sb("ident", [P, P])
        identity(nc, ident)
        with Scope(nc) as c:
            XT = c.sb("XT", [P, TILES, KC, P])
            load_x(nc, x, ident, XT)
            adapter_layer(nc, ident, "l0", w0, ids0, w0.shape[0], x_tiles, x1, XT)
            expert_layer(nc, ident, W, Wr, A, Bm, ids1, x1, x2, XT)
            adapter_layer(nc, ident, "l2", w2, ids2, w2.shape[0], x2, x3, XT)
            XH, XL = (c.sb(name, [P, TILES, KC, P], F32R) for name in ("XH", "XL"))
            split(nc, XT, XH, XL)
            straight, crossed = (c.sb(name, [P, 2, TILES, 2, DH // 2]) for name in ("straight", "crossed"))
            rope_tables(nc, lens, q_norm_w, k_norm_w, straight, crossed)
            project(nc, ident, XH, XL, straight, crossed, Wq, Wk, Wv, qT, kT_own, v_own)
        cache_keys(nc, ident, k_cache, kT_pages)
        attention(nc, ident, table, lens, qT, kT_pages, kT_own, v_cache,
                  v_own.rearrange("t (j s) c m -> (t j) s (c m)", j=BPT), oT)
        output_layer(nc, ident, Wo, oT, x3, out_tiles)


INPUTS = ["x", "itok_B_1_14", "itok_B_0_7", "itok_B_3_7", "itok_Bx16_0_63", "itok_B_207_1644", "L0_cond_weight",
          "L1_cond_W", "L1_cond_Wr", "L1_cond_A", "L1_cond_B", "L2_cond_weight", "L3_cond_Wq", "L3_cond_Wk",
          "L3_cond_Wv", "L3_cond_Wo", "L3_cond_q_norm_w", "L3_cond_k_norm_w", "L3_cond_k_cache",
          "L3_cond_v_cache"]


def kernel(**inputs):
    import concourse.bacc as bacc
    from concourse.bass_utils import run_bass_kernel_spmd

    nc = bacc.Bacc("TRN2", target_bir_lowering=False, num_devices=1)
    arrays, args = {}, []
    for name in INPUTS:
        a = np.ascontiguousarray(inputs[name])
        arrays[f"in_{name}"] = a
        args.append(nc.dram_tensor(f"in_{name}", a.shape, mybir.dt.from_np(a.dtype), kind="ExternalInput").ap())
    args.append(nc.dram_tensor("out", (B, S, D), F32, kind="ExternalOutput").ap())
    build(nc, *args)
    return run_bass_kernel_spmd(nc, [arrays], core_ids=[0]).results[0]["out"]
```

```python
import math
from contextlib import ExitStack

import numpy as np

import concourse.bass as bass
from concourse import mybir

F32 = mybir.dt.float32
F32R = mybir.dt.float32r
I32 = mybir.dt.int32
U32 = mybir.dt.uint32
ALU = mybir.AluOpType
ACT = mybir.ActivationFunctionType
AX = mybir.AxisListType
ds = bass.ds

P = 128
B, S, D = 64, 32, 512
T = B * S
KC = D // P
TILES = T // P
BPT = P // S
E, R = 8, 16
DH, HQ, HK = 128, 32, 8
G = HQ // HK
PAGES, PSIZE, NPP = 64, 32, 16
L = NPP * PSIZE
THETA, EPS = 10000.0, 1e-6
SCALE = 1.0 / math.sqrt(DH)
LANG_BIAS, SCALING = 5.0, 2.0
MASKED = -1e30


class Scope:

    def __init__(self, nc):
        self.nc, self.ctx = nc, ExitStack()

    def __enter__(self):
        self.ctx.__enter__()
        return self

    def __exit__(self, *a):
        return self.ctx.__exit__(*a)

    def sb(self, name, shape, dt=F32):
        return self.ctx.enter_context(self.nc.sbuf_tensor(name, shape, dt))

    def ps(self, name, shape, dt=F32):
        return self.ctx.enter_context(self.nc.psum_tensor(name, shape, dt))

    def sem(self, name):
        return self.ctx.enter_context(self.nc.semaphore(name))

    def block(self):
        return self.ctx.enter_context(self.nc.Block())


def loaded_numbers(nc, engine, source, n):
    return nc.values_load_multi_w_load_instructions(source, engines=(engine,), min_val=0, max_val=n - 1)[1]


def identity(nc, ident):
    with Scope(nc) as c:
        zeroed, made = c.sem("ident_zeroed"), c.sem("ident_made")
        block = c.block()

        @block.gpsimd
        def _(pool):
            nc.gpsimd.memset(ident[:], 0.0).then_inc(zeroed, 1)
            pool.wait_ge(zeroed, 1)
            nc.gpsimd.affine_select(out=ident[:], in_=ident[:], compare_op=ALU.not_equal, fill=1.0,
                                    base=0, pattern=[[-1, P]], channel_multiplier=1).then_inc(made, 1)
            pool.wait_ge(made, 1)


def load_x(nc, x, ident, XT):
    with Scope(nc) as c:
        nat = c.sb("x_nat", [P, 4, D])
        ps = c.ps("x_ps", [P, 2, D])
        loaded = [c.sem(f"x_loaded{s}") for s in range(4)]
        turned, kept = c.sem("x_turned"), c.sem("x_kept")
        tiles = x.rearrange("(t j) s d -> t (j s) d", j=BPT)
        block = c.block()

        @block.sync
        def _(sp):
            for t in range(4):
                sp.dma_start(nat[:, t, :], tiles[t]).then_inc(loaded[t], 16)
            with nc.sync.Fori(0, TILES // 4 - 1) as i:
                for s in range(4):
                    sp.wait_ge(turned, i * 4 + (s + 1))
                    sp.dma_start(nat[:, s, :], tiles[i * 4 + (s + 4)]).then_inc(loaded[s], 16)

        @block.tensor
        def _(pe):
            with nc.tensor.Fori(0, TILES // 4) as i:
                for s in range(4):
                    pe.wait_ge(loaded[s], i * 16 + 16)
                    pe.wait_ge(kept, i * 4 + (s + 1))
                    for k in range(KC):
                        last = nc.tensor.transpose(ps[:, s % 2, k * P:(k + 1) * P],
                                                   nat[:, s, k * P:(k + 1) * P], ident[:])
                    last.then_inc(turned, 1)

        @block.vector
        def _(dve):
            dve.sem_inc(kept, 2)
            with nc.vector.Fori(0, TILES // 4) as i:
                for s in range(4):
                    dve.wait_ge(turned, i * 4 + (s + 1))
                    nc.vector.tensor_copy(XT[:, ds(i * 4 + s, 1), :, :],
                                          ps[:, s % 2, :]).then_inc(kept, 1)


def transposed_weights(nc, ident, name, source, n, WT, beside=None):
    with Scope(nc) as c:
        nat = c.sb(f"{name}_nat", [P, 2, KC, D])
        ps = c.ps(f"{name}_ps", [P, 2, KC, D])
        loaded = [c.sem(f"{name}_loaded{s}") for s in range(2)]
        turned = c.sem(f"{name}_turned")
        kept = [c.sem(f"{name}_kept{half}") for half in range(2)]
        block = c.block()

        @block.sync
        def _(sp):
            for s in range(2):
                sp.dma_start(nat[:, s, :, :], source(s)).then_inc(loaded[s], 16)
            if beside:
                beside["sync"](sp)
            with nc.sync.Fori(0, n // 2 - 1) as i:
                for s in range(2):
                    sp.wait_ge(turned, i * 2 + (s + 1))
                    sp.dma_start(nat[:, s, :, :], source(i * 2 + (s + 2))).then_inc(loaded[s], 16)

        @block.tensor
        def _(pe):
            with nc.tensor.Fori(0, n // 2) as i:
                for s in range(2):
                    pe.wait_ge(loaded[s], i * 16 + 16)
                    for half in range(2):
                        pe.wait_ge(kept[half], i * 2 + (s + 1))
                    for k in range(KC):
                        for o in range(KC):
                            last = nc.tensor.transpose(ps[:, s, k, o * P:(o + 1) * P],
                                                       nat[:, s, o, k * P:(k + 1) * P], ident[:])
                    last.then_inc(turned, 1)

        def keep(copy, i, s, half):
            rows = slice(half * 2, half * 2 + 2)
            copy(WT[:, ds(i * 2 + s, 1), rows, :], ps[:, s, rows, :]).then_inc(kept[half], 1)

        @block.vector
        def _(dve):
            if beside:
                beside["vector"](dve)
                return
            dve.sem_inc(kept[0], 2)
            with nc.vector.Fori(0, n // 2) as i:
                for s in range(2):
                    dve.wait_ge(turned, i * 2 + (s + 1))
                    keep(nc.vector.tensor_copy, i, s, 0)

        @block.scalar
        def _(act):
            if beside:
                act.sem_inc(kept[0], 2)
            act.sem_inc(kept[1], 2)
            for part in range(2):
                with nc.scalar.Fori(n // 4 * part, n // 4 * (part + 1)) as i:
                    for s in range(2):
                        act.wait_ge(turned, i * 2 + (s + 1))
                        if beside:
                            keep(nc.scalar.copy, i, s, 0)
                        keep(nc.scalar.copy, i, s, 1)
                if beside and part == 0:
                    beside["scalar"](act)

        @block.gpsimd
        def _(pool):
            if beside:
                beside["gpsimd"](pool)


def adapter_layer(nc, ident, name, weight, ids, n, x_in, x_out, XT, beside=None):
    with Scope(nc) as outer:
        WT = outer.sb(f"{name}_WT", [P, n, KC, D])
        by_rows = weight.rearrange("a (o p) k -> a p o k", p=P)
        with Scope(nc) as c:
            transposed_weights(nc, ident, f"{name}w", lambda a: by_rows[a], n, WT, beside and beside(c))

        with Scope(nc) as c:
            ids_sb = c.sb(f"{name}_ids", [1, B], I32)
            w_slot = c.sb(f"{name}_w_slot", [P, KC, BPT, D])
            x_slot = c.sb(f"{name}_x_slot", [P, 2, KC, P])
            x_row, y_row = c.sb(f"{name}_x_row", [P, 2, D]), c.sb(f"{name}_y_row", [P, 2, D])
            ps, psT = c.ps(f"{name}_ps", [P, 2, D]), c.ps(f"{name}_psT", [P, 2, D])
            ids_loaded = c.sem(f"{name}_ids_loaded")
            x_loaded = [c.sem(f"{name}_x_loaded{r}") for r in range(2)]
            stored = [c.sem(f"{name}_stored{r}") for r in range(2)]
            x_copied = c.sem(f"{name}_x_copied")
            w_dve, w_act = c.sem(f"{name}_w_dve"), c.sem(f"{name}_w_act")
            slots_free = c.sem(f"{name}_slots_free")
            added, turned, kept = c.sem(f"{name}_added"), c.sem(f"{name}_turned"), c.sem(f"{name}_kept")
            block = c.block()

            @block.sync
            def _(sp):
                sp.dma_start(ids_sb[:], ids.rearrange("(a b) -> a b", a=1)).then_inc(ids_loaded, 16)
                for r in range(2):
                    sp.sem_inc(stored[r], 16)
                    sp.dma_start(x_row[:, r, :], x_in[r]).then_inc(x_loaded[r], 16)

                def store(t, r):
                    sp.wait_ge(added, t + 1)
                    sp.dma_start(x_out[t], y_row[:, r, :]).then_inc(stored[r], 16)

                with nc.sync.Fori(0, TILES // 2 - 1) as i:
                    for r in range(2):
                        store(i * 2 + r, r)
                        sp.dma_start(x_row[:, r, :], x_in[i * 2 + (r + 2)]).then_inc(x_loaded[r], 16)
                for r in range(2):
                    store(TILES - 2 + r, r)
                for r in range(2):
                    sp.wait_ge(stored[r], 16 * (TILES // 2 + 1))

            @block.gpsimd
            def _(pool):
                for t in range(2):
                    nc.gpsimd.tensor_copy(x_slot[:, t, :, :], XT[:, t, :, :]).then_inc(x_copied, 1)
                with nc.gpsimd.Fori(1, TILES // 2) as i:
                    for r in range(2):
                        pool.wait_ge(slots_free, i * (2 * KC) + KC * r)
                        nc.gpsimd.tensor_copy(x_slot[:, r, :, :], XT[:, ds(i * 2 + r, 1), :, :]).then_inc(x_copied, 1)

            def adapters(engine, t):
                return loaded_numbers(nc, engine, ids_sb[0:1, ds(t * BPT, BPT)], n)

            def weights(eng, move, t, regs, chunks, mine, sem):
                for k in chunks:
                    eng.wait_ge(slots_free, t * KC + (k + 1))
                    for j in mine:
                        last = move(w_slot[:, k, j, :], WT[:, ds(regs[j], 1), k, :])
                    last.then_inc(sem, 1)

            ALL = tuple(range(KC))

            @block.scalar
            def _(act):
                mine = (2, 3)
                act.sem_inc(kept, 2)
                act.wait_ge(ids_loaded, 16)

                def keep(t, r):
                    act.wait_ge(turned, t + 1)
                    nc.scalar.copy(XT[:, ds(t, 1), :, :], psT[:, r, :]).then_inc(kept, 1)

                for t in range(2):
                    weights(act, nc.scalar.copy, t, adapters(mybir.EngineType.Activation, t), ALL, mine, w_act)
                with nc.scalar.Fori(0, TILES // 2 - 1) as i:
                    for r in range(2):
                        t = i * 2 + r
                        regs = adapters(mybir.EngineType.Activation, i * 2 + (r + 2))
                        weights(act, nc.scalar.copy, i * 2 + (r + 2), regs, ALL[:2], mine, w_act)
                        keep(t, r)
                        weights(act, nc.scalar.copy, i * 2 + (r + 2), regs, ALL[2:], mine, w_act)
                keep(TILES - 2, 0)
                keep(TILES - 1, 1)

            @block.vector
            def _(dve):
                mine = (0, 1)
                dve.wait_ge(ids_loaded, 16)

                def add(t, i, r):
                    dve.wait_ge(slots_free, t * KC + 2 * KC)
                    dve.wait_ge(x_loaded[r], i * 16 + 16)
                    dve.wait_ge(stored[r], i * 16 + 16)
                    nc.vector.tensor_tensor(y_row[:, r, :], ps[:, r, :], x_row[:, r, :], ALU.add).then_inc(added, 1)

                for t in range(2):
                    weights(dve, nc.vector.tensor_copy, t, adapters(mybir.EngineType.DVE, t), ALL, mine, w_dve)
                with nc.vector.Fori(0, TILES // 2 - 1) as i:
                    for r in range(2):
                        add(i * 2 + r, i, r)
                        regs = adapters(mybir.EngineType.DVE, i * 2 + (r + 2))
                        weights(dve, nc.vector.tensor_copy, i * 2 + (r + 2), regs, ALL, mine, w_dve)
                add(TILES - 2, TILES // 2 - 1, 0)
                add(TILES - 1, TILES // 2 - 1, 1)

            @block.tensor
            def _(pe):
                pe.sem_inc(slots_free, KC)

                def products(t, r, chunks):
                    if 0 in chunks:
                        pe.wait_ge(x_copied, t + 1)
                    for k in chunks:
                        pe.wait_ge(w_dve, t * KC + (k + 1))
                        pe.wait_ge(w_act, t * KC + (k + 1))
                        for j in range(BPT):
                            rows = slice(j * S, (j + 1) * S)
                            last = nc.tensor.matmul(ps[rows, r, :], x_slot[:, r, k, rows], w_slot[:, k, j, :],
                                                    start=k == 0, stop=k == KC - 1)
                        last.then_inc(slots_free, 1)

                def turn(t, r):
                    pe.wait_ge(added, t + 1)
                    pe.wait_ge(kept, t + 1)
                    for k in range(KC):
                        last = nc.tensor.transpose(psT[:, r, k * P:(k + 1) * P], y_row[:, r, k * P:(k + 1) * P],
                                                   ident[:])
                    last.then_inc(turned, 1)

                products(0, 0, ALL)
                products(1, 1, ALL[:2])
                with nc.tensor.Fori(0, TILES // 2 - 1) as i:
                    for r in range(2):
                        turn(i * 2 + r, r)
                        products(i * 2 + (r + 1), 1 - r, ALL[2:])
                        products(i * 2 + (r + 2), r, ALL[:2])
                turn(TILES - 2, 0)
                products(TILES - 1, 1, ALL[2:])
                turn(TILES - 1, 1)


def expert_layer(nc, ident, W, Wr, A, Bm, ids, x_in, x_out, XT):
    ER = E * R
    with Scope(nc) as outer:
        WT = outer.sb("l1_WT", [P, KC, D])
        AT = outer.sb("l1_AT", [P, KC, ER + E])
        BT = outer.sb("l1_BT", [P, D])
        H = outer.sb("l1_H", [P, TILES, ER])
        HT = outer.sb("l1_HT", [P, TILES, P])
        logits = outer.sb("l1_logits", [P, TILES, E])
        lang = outer.sb("l1_lang", [P, TILES], I32)

        with Scope(nc) as c:
            Wn, An = c.sb("l1_Wn", [P, KC, D]), c.sb("l1_An", [P, D])
            Wrn, Bn = c.sb("l1_Wrn", [E, D]), c.sb("l1_Bn", [P, KC, ER])
            ps = c.ps("l1_wps", [P, 7, D])
            loaded, turned, kept = c.sem("l1_loaded"), c.sem("l1_turned"), c.sem("l1_kept")
            lang_loaded = c.sem("l1_lang_loaded")
            block = c.block()

            @block.sync
            def _(sp):
                sp.dma_start(Wn[:], W.rearrange("(o p) k -> p o k", p=P)).then_inc(loaded, 16)
                sp.dma_start(An[:], A.rearrange("e r k -> (e r) k")).then_inc(loaded, 16)
                sp.dma_start(Wrn[:], Wr).then_inc(loaded, 16)
                for o in range(KC):
                    sp.dma_start(Bn[:, o, :].rearrange("p (e r) -> p e r", e=E),
                                 Bm[:, o * P:(o + 1) * P, :].rearrange("e p r -> p e r")).then_inc(loaded, 16)
                by_tile = ids.rearrange("(t j) -> j t", j=BPT)
                for j in range(BPT):
                    sp.dma_start(lang[j * S:(j + 1) * S, :],
                                 by_tile[j:j + 1, :].broadcast_to([S, TILES]),
                                 allow_slow_non_contiguous=True).then_inc(lang_loaded, 16)
                sp.wait_ge(lang_loaded, 16 * BPT)

            @block.tensor
            def _(pe):
                pe.wait_ge(loaded, 16 * (3 + KC))
                for k in range(KC):
                    for o in range(KC):
                        nc.tensor.transpose(ps[:, k, o * P:(o + 1) * P], Wn[:, o, k * P:(k + 1) * P], ident[:])
                for k in range(KC):
                    nc.tensor.transpose(ps[:, 4, k * P:(k + 1) * P], An[:, k * P:(k + 1) * P], ident[:])
                for k in range(KC):
                    nc.tensor.transpose(ps[:, 5, k * E:(k + 1) * E], Wrn[:, k * P:(k + 1) * P], ident[0:E, 0:E])
                for o in range(KC):
                    last = nc.tensor.transpose(ps[:, 6, o * P:(o + 1) * P], Bn[:, o, :], ident[:])
                last.then_inc(turned, 1)

            @block.vector
            def _(dve):
                dve.wait_ge(turned, 1)
                nc.vector.tensor_copy(WT[:], ps[:, 0:KC, :])
                nc.vector.tensor_copy(AT[:, :, 0:ER], ps[:, 4, :].rearrange("p (k e) -> p k e", k=KC))
                nc.vector.tensor_copy(AT[:, :, ER:], ps[:, 5, 0:KC * E].rearrange("p (k e) -> p k e", k=KC))
                nc.vector.tensor_copy(BT[:], ps[:, 6, :]).then_inc(kept, 1)
                dve.wait_ge(kept, 1)

        with Scope(nc) as c:
            ps = c.ps("l1_hps", [P, 2, 512])
            done, banks_free = c.sem("l1_h_done"), c.sem("l1_h_free")
            block = c.block()

            @block.tensor
            def _(pe):
                for t in range(TILES):
                    pe.wait_ge(banks_free, t + 1)
                    for k in range(KC):
                        last = nc.tensor.matmul(ps[:, t % 2, 0:ER + E], XT[:, t, k, :], AT[:, k, :],
                                                start=k == 0, stop=k == KC - 1)
                    last.then_inc(done, 1)

            @block.vector
            def _(dve):
                dve.sem_inc(banks_free, 2)
                with nc.vector.Fori(0, TILES // 2) as i:
                    for r in range(2):
                        dve.wait_ge(done, i * 2 + (r + 1))
                        nc.vector.tensor_copy(logits[:, ds(i * 2 + r, 1), :], ps[:, r, ER:ER + E])
                        nc.vector.tensor_copy(H[:, ds(i * 2 + r, 1), :], ps[:, r, 0:ER]).then_inc(banks_free, 1)

        with Scope(nc) as c:
            iota = c.sb("l1_iota", [P, E])
            langf = c.sb("l1_langf", [P, TILES])
            hot = c.sb("l1_hot", [P, TILES, E])
            top, topi = c.sb("l1_top", [P, TILES, 8]), c.sb("l1_topi", [P, TILES, 8], U32)
            topf = c.sb("l1_topf", [P, TILES, 8])
            diff, ex, w1, w2 = (c.sb(f"l1_{x}", [P, TILES]) for x in ("diff", "ex", "w1", "w2"))
            g1, g2 = c.sb("l1_g1", [P, TILES, E]), c.sb("l1_g2", [P, TILES, E])
            chain, exp_done = c.sem("l1_chain"), c.sem("l1_exp")
            block = c.block()
            each = lambda x: x.unsqueeze(2).broadcast_to([P, TILES, E])
            iota_all = iota[:].unsqueeze(1).broadcast_to([P, TILES, E])

            @block.vector
            def _(dve):
                steps = [0]

                def link(ins):
                    steps[0] += 1
                    ins.then_inc(chain, 1)
                    dve.wait_ge(chain, steps[0])

                for e in range(E):
                    nc.vector.memset(iota[:, e:e + 1], float(e))
                link(nc.vector.tensor_copy(langf[:], lang[:]))
                link(nc.vector.tensor_tensor(hot[:], each(langf[:]), iota_all, ALU.is_equal))
                link(nc.vector.scalar_tensor_tensor(out=logits[:], in0=hot[:], scalar=LANG_BIAS, in1=logits[:],
                                                    op0=ALU.mult, op1=ALU.add))
                for t in range(TILES):
                    last = nc.vector.max(top[:, t, :], logits[:, t, :])
                link(last)
                for t in range(TILES):
                    last = nc.vector.max_index(topi[:, t, :], top[:, t, :], logits[:, t, :])
                link(last)
                nc.vector.tensor_copy(topf[:], topi[:])
                link(nc.vector.tensor_tensor(diff[:], top[:, :, 1], top[:, :, 0], ALU.subtract))
                dve.wait_ge(exp_done, 1)
                link(nc.vector.tensor_scalar(w1[:], ex[:], 1.0, None, ALU.add))
                link(nc.vector.reciprocal(w1[:], w1[:]))
                link(nc.vector.tensor_tensor(w2[:], ex[:], w1[:], ALU.mult))
                nc.vector.tensor_tensor(g1[:], each(topf[:, :, 0]), iota_all, ALU.is_equal)
                link(nc.vector.tensor_tensor(g2[:], each(topf[:, :, 1]), iota_all, ALU.is_equal))
                nc.vector.tensor_tensor(g1[:], g1[:], each(w1[:]), ALU.mult)
                link(nc.vector.tensor_tensor(g2[:], g2[:], each(w2[:]), ALU.mult))
                link(nc.vector.tensor_tensor(g1[:], g1[:], g2[:], ALU.add))
                link(nc.vector.tensor_scalar(g1[:], g1[:], SCALING, None, ALU.mult))
                h = H[:].rearrange("p t (e r) -> p (t e) r", r=R)
                gates = g1[:].rearrange("p t e -> p (t e)").unsqueeze(2).broadcast_to([P, TILES * E, R])
                link(nc.vector.tensor_tensor(h, h, gates, ALU.mult))

            @block.scalar
            def _(act):
                act.wait_ge(chain, 6)
                nc.scalar.activation(ex[:], diff[:], ACT.Exp).then_inc(exp_done, 1)

        with Scope(nc) as c:
            ps, psT = c.ps("l1_ps", [P, 2, D]), c.ps("l1_psT", [P, 4, D])
            x_row, y_row = c.sb("l1_x_row", [P, 2, D]), c.sb("l1_y_row", [P, 2, D])
            x_loaded = [c.sem(f"l1_x_loaded{r}") for r in range(2)]
            stored = [c.sem(f"l1_stored{r}") for r in range(2)]
            h_turned, h_kept = c.sem("l1_h_turned"), c.sem("l1_h_kept")
            done, added, turned, kept = (c.sem(f"l1_{x}") for x in ("done", "added", "turned", "kept"))
            block = c.block()

            @block.sync
            def _(sp):
                for t in range(2):
                    sp.dma_start(x_row[:, t, :], x_in[t]).then_inc(x_loaded[t], 16)
                for t in range(TILES):
                    sp.wait_ge(added, t + 1)
                    sp.dma_start(x_out[t], y_row[:, t % 2, :]).then_inc(stored[t % 2], 16)
                    if t + 2 < TILES:
                        sp.dma_start(x_row[:, t % 2, :], x_in[t + 2]).then_inc(x_loaded[t % 2], 16)
                for r in range(2):
                    sp.wait_ge(stored[r], 16 * (TILES // 2))

            @block.tensor
            def _(pe):
                for t in range(TILES):
                    last = nc.tensor.transpose(psT[:, t // 4, (t % 4) * P:(t % 4 + 1) * P], H[:, t, :], ident[:])
                last.then_inc(h_turned, 1)
                pe.wait_ge(h_kept, 1)

                def turn(t):
                    pe.wait_ge(added, t + 1)
                    if t >= 2:
                        pe.wait_ge(kept, t - 1)
                    for k in range(KC):
                        last = nc.tensor.transpose(psT[:, t % 2, k * P:(k + 1) * P],
                                                   y_row[:, t % 2, k * P:(k + 1) * P], ident[:])
                    last.then_inc(turned, 1)

                for t in range(TILES):
                    for k in range(KC):
                        nc.tensor.matmul(ps[:, t % 2, :], XT[:, t, k, :], WT[:, k, :], start=k == 0, stop=False)
                    nc.tensor.matmul(ps[:, t % 2, :], HT[:, t, :], BT[:], start=False, stop=True).then_inc(done, 1)
                    if t >= 1:
                        turn(t - 1)
                turn(TILES - 1)

            @block.vector
            def _(dve):
                dve.wait_ge(h_turned, 1)
                nc.vector.tensor_copy(HT[:], psT[:]).then_inc(h_kept, 1)
                for t in range(TILES):
                    dve.wait_ge(done, t + 1)
                    dve.wait_ge(x_loaded[t % 2], 16 * (t // 2 + 1))
                    dve.wait_ge(stored[t % 2], 16 * (t // 2))
                    nc.vector.tensor_tensor(y_row[:, t % 2, :], ps[:, t % 2, :], x_row[:, t % 2, :],
                                            ALU.add).then_inc(added, 1)

            @block.scalar
            def _(act):
                for t in range(TILES):
                    act.wait_ge(turned, t + 1)
                    nc.scalar.copy(XT[:, t, :, :], psT[:, t % 2, :]).then_inc(kept, 1)


def cache_keys(nc, ident, k_cache, resident):
    with Scope(nc) as c:
        PG = P // PSIZE
        n = PAGES // PG
        nat = c.sb("kc_nat", [P, 4, HK * DH])
        ps = c.ps("kc_ps", [P, 2, 2, 512])
        loaded = [c.sem(f"kc_loaded{s}") for s in range(4)]
        turned = c.sem("kc_turned")
        kept_dve, kept_act = c.sem("kc_kept_dve"), c.sem("kc_kept_act")
        rows = k_cache.rearrange("(n g) k h d -> n (g k) (h d)", g=PG)
        block = c.block()

        @block.sync
        def _(sp):
            for s in range(4):
                sp.dma_start(nat[:, s, :], rows[s]).then_inc(loaded[s], 16)
            with nc.sync.Fori(0, n // 4 - 1) as i:
                for s in range(4):
                    sp.wait_ge(turned, i * 4 + (s + 1))
                    sp.dma_start(nat[:, s, :], rows[i * 4 + (s + 4)]).then_inc(loaded[s], 16)

        @block.tensor
        def _(pe):
            with nc.tensor.Fori(0, n // 4) as i:
                for s in range(4):
                    pe.wait_ge(loaded[s], i * 16 + 16)
                    pe.wait_ge(kept_dve, i * 4 + (s + 1))
                    pe.wait_ge(kept_act, i * 4 + (s + 1))
                    for h in range(HK):
                        last = nc.tensor.transpose(ps[:, s % 2, h // 4, (h % 4) * P:(h % 4 + 1) * P],
                                                   nat[:, s, h * DH:(h + 1) * DH], ident[:])
                    last.then_inc(turned, 1)

        def halves(m, s, half):
            return (resident[:, ds(m * PG, PG), half * 4:half * 4 + 4, :].rearrange("p g h k -> p h g k"),
                    ps[:, s, half, :].rearrange("p (h g k) -> p h g k", h=4, g=PG))

        @block.vector
        def _(dve):
            dve.sem_inc(kept_dve, 2)
            with nc.vector.Fori(0, n // 2) as i:
                for s in range(2):
                    dve.wait_ge(turned, i * 2 + (s + 1))
                    nc.vector.tensor_copy(*halves(i * 2 + s, s, 0)).then_inc(kept_dve, 1)

        @block.scalar
        def _(act):
            act.sem_inc(kept_act, 2)
            with nc.scalar.Fori(0, n // 2) as i:
                for s in range(2):
                    act.wait_ge(turned, i * 2 + (s + 1))
                    nc.scalar.copy(*halves(i * 2 + s, s, 1)).then_inc(kept_act, 1)

def lane_lengths(sp, lens, out, sem):
    by_tile = lens.rearrange("(t j) -> j t", j=BPT)
    for j in range(BPT):
        sp.dma_start(out[j * S:(j + 1) * S, :], by_tile[j:j + 1, :].broadcast_to([S, TILES]),
                     allow_slow_non_contiguous=True).then_inc(sem, 16)


def rope_tables(nc, c, lens, q_norm_w, k_norm_w, straight, crossed):
    HALF = DH // 2
    inv_freq = (np.float32(1.0) / np.float32(THETA) ** (np.arange(0, DH, 2, dtype=np.float32) / np.float32(DH)))
    TWO_PI_A = 6.28125
    TWO_PI_B = float(np.float32(round((2 * math.pi - TWO_PI_A) * 2 ** 21) / 2 ** 21))
    TWO_PI_C = 2 * math.pi - TWO_PI_A - TWO_PI_B
    ROUND = 1.5 * 2 ** 23
    PI_BELOW = 3.1415925
    leni, lane = c.sb("rt_leni", [P, TILES], I32), c.sb("rt_lane", [P, 1], I32)
    pos, lanef = c.sb("rt_pos", [P, TILES]), c.sb("rt_lanef", [P, 1])
    inv = c.sb("rt_inv", [P, HALF])
    ang, turns = c.sb("rt_ang", [P, TILES, HALF]), c.sb("rt_turns", [P, TILES, HALF])
    cos, sin = c.sb("rt_cos", [P, TILES, HALF]), c.sb("rt_sin", [P, TILES, HALF])
    w = [c.sb("rt_wq", [P, DH]), c.sb("rt_wk", [P, DH])]
    loaded, lane_made = c.sem("rt_loaded"), c.sem("rt_lane_made")
    chain, reduced, looked_up = c.sem("rt_chain"), c.sem("rt_reduced"), c.sem("rt_looked_up")

    def sync(sp):
        lane_lengths(sp, lens, leni, loaded)
        for x, src in zip(w, (q_norm_w, k_norm_w)):
            sp.dma_start(x[:], src.rearrange("(a d) -> a d", a=1).broadcast_to([P, DH])).then_inc(loaded, 16)

    def gpsimd(pool):
        for j in range(BPT):
            nc.gpsimd.iota(lane[j * S:(j + 1) * S, :], pattern=[[0, 1]], base=0,
                           channel_multiplier=1).then_inc(lane_made, 1)
            pool.wait_ge(lane_made, j + 1)

    def vector(dve):
        steps = [0]

        def link(ins):
            steps[0] += 1
            ins.then_inc(chain, 1)
            dve.wait_ge(chain, steps[0])

        for i in range(HALF):
            nc.vector.memset(inv[:, i:i + 1], float(inv_freq[i]))
        dve.wait_ge(lane_made, BPT)
        dve.wait_ge(loaded, 16 * (BPT + 2))
        nc.vector.tensor_copy(lanef[:], lane[:])
        link(nc.vector.tensor_copy(pos[:], leni[:]))
        link(nc.vector.tensor_scalar(pos[:], pos[:], lanef[:, 0:1], None, ALU.add))
        link(nc.vector.tensor_tensor(ang[:], pos[:].unsqueeze(2).broadcast_to([P, TILES, HALF]),
                                     inv[:].unsqueeze(1).broadcast_to([P, TILES, HALF]), ALU.mult))
        link(nc.vector.tensor_scalar(turns[:], ang[:], 1.0 / (2 * math.pi), None, ALU.mult))
        link(nc.vector.tensor_scalar(turns[:], turns[:], ROUND, None, ALU.add))
        link(nc.vector.tensor_scalar(turns[:], turns[:], -ROUND, None, ALU.add))
        for part in (TWO_PI_A, TWO_PI_B, TWO_PI_C):
            link(nc.vector.scalar_tensor_tensor(out=ang[:], in0=turns[:], scalar=-part, in1=ang[:],
                                                op0=ALU.mult, op1=ALU.add))
        link(nc.vector.tensor_scalar(ang[:], ang[:], PI_BELOW, -PI_BELOW, ALU.min, ALU.max))
        link(nc.vector.tensor_scalar(turns[:], ang[:], -1.0, None, ALU.mult))
        link(nc.vector.tensor_tensor(turns[:], turns[:], ang[:], ALU.min))
        nc.vector.tensor_scalar(turns[:], turns[:], math.pi / 2, None, ALU.add).then_inc(reduced, 1)
        dve.wait_ge(looked_up, 2)
        for kind in range(2):
            for out, table, order in ((straight, cos, (0, 1)), (crossed, sin, (1, 0))):
                for half in range(2):
                    wh = w[kind][:, order[half] * HALF:(order[half] + 1) * HALF]
                    sign = -1.0 if out is crossed and half == 0 else 1.0
                    nc.vector.scalar_tensor_tensor(out=out[:, kind, :, half, :], in0=table[:], scalar=sign,
                                                   in1=wh.unsqueeze(1).broadcast_to([P, TILES, HALF]),
                                                   op0=ALU.mult, op1=ALU.mult)

    def scalar(act):
        act.wait_ge(reduced, 1)
        nc.scalar.activation(sin[:], ang[:], ACT.Sin).then_inc(looked_up, 1)
        nc.scalar.activation(cos[:], turns[:], ACT.Sin).then_inc(looked_up, 1)

    return {"sync": sync, "gpsimd": gpsimd, "vector": vector, "scalar": scalar}


def project(nc, ident, XT, XH, XL, straight, crossed, Wq, Wk, Wv, qT, kT_own, v_own):
    CQ, CK = HQ // 4, HK // 4
    CHUNKS = CQ + 2 * CK
    FIRST_K, FIRST_V = CQ, CQ + CK
    LOOPED = CQ - 2
    HALF = DH // 2
    W_AFTER, LOW_AFTER = (TILES - 5, TILES - 3), (TILES - 2, TILES - 1)
    AHEAD = 4

    def kind(chunk):
        if not isinstance(chunk, int) or chunk < FIRST_K:
            return 0
        return 1 if chunk < FIRST_V else 2

    def chunks(eng, body):
        with eng.Fori(0, LOOPED // 2) as i:
            for s in range(2):
                body(i * 2 + s, s)
        for chunk in range(LOOPED, CHUNKS):
            body(chunk, chunk % 2)

    def known(chunk):
        return isinstance(chunk, int)

    by_rows = [w.rearrange("(c o p) k -> c p o k", p=P, o=KC) for w in (Wq, Wk, Wv)]

    def rows_of(chunk):
        return by_rows[kind(chunk)][chunk - (0, FIRST_K, FIRST_V)[kind(chunk)] if known(chunk) else chunk]

    with Scope(nc) as c:
        nat = c.sb("pr_nat", [P, 2, KC, D])
        WH, WL = c.sb("pr_WH", [P, 2, KC, D], F32R), c.sb("pr_WL", [P, 2, KC, D], F32R)
        junk = c.sb("pr_junk", [P, 4, DH])
        eps = c.sb("pr_eps", [P, 1])
        sums, root = (c.sb(f"pr_{x}", [P, AHEAD, 4]) for x in ("sums", "root"))
        rstd = c.sb("pr_rstd", [P, 2, 4])
        u, m1, m2, y = (c.sb(f"pr_{x}", [P, 2, 4, 2, HALF]) for x in ("u", "m1", "m2", "y"))
        turned_out = c.sb("pr_turned_out", [P, 2, BPT, 4, S])
        v_out = c.sb("pr_v_out", [P, AHEAD, D])
        psW = c.ps("pr_psW", [P, KC // 2, D])
        ps, psT = c.ps("pr_ps", [P, AHEAD, D]), c.ps("pr_psT", [P, 2, D])
        w_loaded = [c.sem(f"pr_w_loaded{s}") for s in range(2)]
        w_turned, w_high, w_low = c.sem("pr_w_turned"), c.sem("pr_w_high"), c.sem("pr_w_low")
        eps_made = c.sem("pr_eps_made")
        x_high, x_low = c.sem("pr_x_high"), c.sem("pr_x_low")
        done = c.sem("pr_done")
        squared, rooted, scaled = c.sem("pr_squared"), c.sem("pr_rooted"), c.sem("pr_scaled")
        inverted = c.sem("pr_inverted")
        straight_done, crossed_done, summed = c.sem("pr_straight"), c.sem("pr_crossed"), c.sem("pr_summed")
        turned, kept = c.sem("pr_turned"), c.sem("pr_kept")
        v_kept = c.sem("pr_v_kept")
        stored = [c.sem(f"pr_stored{s}") for s in range(2)]
        v_stored = [c.sem(f"pr_v_stored{s}") for s in range(AHEAD)]
        block = c.block()

        @block.sync
        def _(sp):
            for s in range(2):
                sp.sem_inc(stored[s], 16)
                sp.dma_start(nat[:, s, :, :], rows_of(s)).then_inc(w_loaded[s], 16)

            def body(chunk, s):
                if not known(chunk) or chunk + 2 < CHUNKS:
                    sp.wait_ge(w_turned, chunk * 2 + 2)
                    sp.dma_start(nat[:, s, :, :], rows_of(chunk + 2)).then_inc(w_loaded[s], 16)
                for t in range(TILES):
                    r = t % 2
                    if kind(chunk) == 2:
                        sp.wait_ge(v_kept, (chunk - FIRST_V) * TILES + t + 1)
                        sp.dma_start(v_own[t, :, chunk - FIRST_V, :], v_out[:, t % AHEAD, :]).then_inc(
                            v_stored[t % AHEAD], 16)
                        continue
                    sp.wait_ge(kept, chunk * TILES + (t + 3))
                    store = (qT[t * BPT:(t + 1) * BPT, :, chunk, :] if kind(chunk) == 0
                             else kT_own[t * BPT:(t + 1) * BPT, :, chunk - FIRST_K, :])
                    sp.dma_start(store.rearrange("j d m -> d j m"),
                                 turned_out[:, r, :, :, :].rearrange("d j g s -> d j (g s)")).then_inc(stored[r], 16)

            chunks(nc.sync, body)
            for r in range(2):
                sp.wait_ge(stored[r], 16 * (FIRST_V * TILES // 2 + 1))
            for a in range(AHEAD):
                sp.wait_ge(v_stored[a], 16 * (CK * TILES // AHEAD))

        @block.tensor
        def _(pe):
            pe.sem_inc(turned, 2)

            def turn_weights(chunk, s, half):
                pe.wait_ge(w_loaded[s], (chunk // 2) * 16 + 16 if known(chunk) else (chunk - s) * 8 + 16)
                if not known(chunk) or chunk + half > 0:
                    pe.wait_ge(w_low, chunk * 2 + half)
                for k in range(KC // 2):
                    for o in range(KC):
                        last = nc.tensor.transpose(psW[:, k, o * P:(o + 1) * P],
                                                   nat[:, s, o, (half * 2 + k) * P:(half * 2 + k + 1) * P], ident[:])
                last.then_inc(w_turned, 1)

            def products(chunk, s, t):
                unit = chunk * TILES + t
                if t == 0:
                    pe.wait_ge(w_low, chunk * 2 + 2)
                if known(chunk) and unit - AHEAD >= FIRST_V * TILES:
                    pe.wait_ge(v_kept, unit - AHEAD + 1 - FIRST_V * TILES)
                elif not known(chunk) or unit >= AHEAD:
                    pe.wait_ge(scaled, unit - (AHEAD - 1))
                for k in range(KC):
                    for n, (x, w) in enumerate(((XH, WH), (XH, WL), (XL, WH))):
                        last = nc.tensor.matmul(ps[:, t % AHEAD, :], x[:, t, k, :], w[:, s, k, :],
                                                start=k == 0 and n == 0, stop=k == KC - 1 and n == 2)
                last.then_inc(done, 1)

            def turn(chunk, t):
                unit = chunk * TILES + t
                pe.wait_ge(summed, unit + 1)
                pe.wait_ge(kept, unit + 1)
                for g in range(4):
                    last = nc.tensor.transpose(psT[:, t % 2, g * P:(g + 1) * P],
                                               y[:, t % 2, g, :, :].rearrange("p a b -> p (a b)"), ident[:])
                last.then_inc(turned, 1)

            def body(chunk, s):
                for t in range(TILES):
                    if t + AHEAD < TILES:
                        products(chunk, s, t + AHEAD)
                    elif not known(chunk) or chunk + 1 < CHUNKS:
                        products(chunk + 1, 1 - s, t + AHEAD - TILES)
                    if kind(chunk) < 2:
                        turn(chunk, t)
                    if t in W_AFTER and (not known(chunk) or chunk + 2 < CHUNKS):
                        turn_weights(chunk + 2, s, W_AFTER.index(t))

            for chunk in range(2):
                for half in range(2):
                    turn_weights(chunk, chunk, half)
            pe.wait_ge(x_low, TILES // 4)
            for t in range(AHEAD):
                products(0, 0, t)
            chunks(nc.tensor, body)

        @block.scalar
        def _(act):
            act.sem_inc(kept, 2)
            act.wait_ge(eps_made, 1)

            def high(chunk, s, half):
                act.wait_ge(w_turned, chunk * 2 + half + 1)
                nc.scalar.copy(WH[:, s, half * 2:half * 2 + 2, :], psW[:]).then_inc(w_high, 1)

            def front(chunk, t):
                unit, r, a = chunk * TILES + t, t % 2, t % AHEAD
                act.wait_ge(done, unit + 1)
                if kind(chunk) == 2:
                    if unit - FIRST_V * TILES >= AHEAD:
                        act.wait_ge(v_stored[a], 16 * ((unit - FIRST_V * TILES) // AHEAD))
                    nc.scalar.copy(v_out[:, a, :], ps[:, a, :]).then_inc(v_kept, 1)
                    return
                for g in range(4):
                    nc.scalar.activation(junk[:, g, :], ps[:, a, g * DH:(g + 1) * DH], ACT.Square,
                                         accum_out=sums[:, a, g:g + 1]).then_inc(squared, 1)
                act.wait_ge(squared, unit * 4 + 4)
                nc.scalar.activation(root[:, a, :], sums[:, a, :], ACT.Sqrt, bias=eps[:],
                                     scale=1.0 / DH).then_inc(rooted, 1)

            def back(chunk, t):
                unit, r = chunk * TILES + t, t % 2
                act.wait_ge(turned, unit + 3)
                act.wait_ge(stored[r], (chunk * (TILES // 2) + (t // 2 + 1)) * 16)
                nc.scalar.copy(turned_out[:, r, :, :, :].rearrange("p j g s -> p g j s"),
                               psT[:, r, :].rearrange("p (g j s) -> p g j s", g=4, j=BPT)).then_inc(kept, 1)

            def body(chunk, s):
                for t in range(TILES):
                    if t + AHEAD < TILES:
                        front(chunk, t + AHEAD)
                    elif not known(chunk) or chunk + 1 < CHUNKS:
                        front(chunk + 1, t + AHEAD - TILES)
                    if kind(chunk) < 2:
                        back(chunk, t)
                    if t in W_AFTER and (not known(chunk) or chunk + 2 < CHUNKS):
                        high(chunk + 2, s, W_AFTER.index(t))

            for t in range(0, TILES, 4):
                nc.scalar.copy(XH[:, t:t + 4, :, :], XT[:, t:t + 4, :, :]).then_inc(x_high, 1)
            for chunk in range(2):
                for half in range(2):
                    high(chunk, chunk, half)
            for t in range(AHEAD):
                front(0, t)
            chunks(nc.scalar, body)

        @block.vector
        def _(dve):
            nc.vector.memset(eps[:], EPS).then_inc(eps_made, 1)

            def low(chunk, s, half):
                dve.wait_ge(w_high, chunk * 2 + half + 1)
                rows = slice(half * 2, half * 2 + 2)
                nc.vector.tensor_tensor(WL[:, s, rows, :], psW[:], WH[:, s, rows, :].bitcast(F32),
                                        ALU.subtract).then_inc(w_low, 1)

            def scale(chunk, t):
                unit, r, kd = chunk * TILES + t, t % 2, kind(chunk)
                dve.wait_ge(rooted, unit + 1)
                nc.vector.reciprocal(rstd[:, r, :], root[:, t % AHEAD, :]).then_inc(inverted, 1)
                dve.wait_ge(inverted, unit + 1)
                nc.vector.tensor_tensor(u[:, r, :, :, :].rearrange("p g a b -> p g (a b)"),
                                        ps[:, t % AHEAD, :].rearrange("p (g d) -> p g d", g=4),
                                        rstd[:, r, :].unsqueeze(2).broadcast_to([P, 4, DH]),
                                        ALU.mult).then_inc(scaled, 1)
                dve.wait_ge(scaled, unit + 1)
                table = straight[:, kd, t, :, :].rearrange("p a b -> p (a b)").unsqueeze(1)
                nc.vector.tensor_tensor(m1[:, r, :, :, :].rearrange("p g a b -> p g (a b)"),
                                        u[:, r, :, :, :].rearrange("p g a b -> p g (a b)"),
                                        table.broadcast_to([P, 4, DH]), ALU.mult).then_inc(straight_done, 1)

            def add(chunk, t):
                unit, r = chunk * TILES + t, t % 2
                dve.wait_ge(straight_done, unit + 1)
                dve.wait_ge(crossed_done, unit + 1)
                dve.wait_ge(turned, unit + 1)
                nc.vector.tensor_tensor(y[:, r, :, :, :], m1[:, r, :, :, :], m2[:, r, :, :, :],
                                        ALU.add).then_inc(summed, 1)

            def body(chunk, s):
                for t in range(TILES):
                    if kind(chunk) < 2:
                        if t + 1 < TILES:
                            scale(chunk, t + 1)
                        elif not known(chunk) or chunk + 1 < FIRST_V:
                            scale(chunk + 1, 0)
                        add(chunk, t)
                    if t in LOW_AFTER and (not known(chunk) or chunk + 2 < CHUNKS):
                        low(chunk + 2, s, LOW_AFTER.index(t))

            for t in range(0, TILES, 4):
                dve.wait_ge(x_high, t // 4 + 1)
                nc.vector.tensor_tensor(XL[:, t:t + 4, :, :], XT[:, t:t + 4, :, :],
                                        XH[:, t:t + 4, :, :].bitcast(F32), ALU.subtract).then_inc(x_low, 1)
            for chunk in range(2):
                for half in range(2):
                    low(chunk, chunk, half)
            scale(0, 0)
            chunks(nc.vector, body)

        @block.gpsimd
        def _(pool):
            def cross(chunk, t):
                unit, r, kd = chunk * TILES + t, t % 2, kind(chunk)
                pool.wait_ge(scaled, unit + 1)
                for half in range(2):
                    table = crossed[:, kd, t, half, :].unsqueeze(1).broadcast_to([P, 4, HALF])
                    last = nc.gpsimd.tensor_tensor(m2[:, r, :, half, :], u[:, r, :, 1 - half, :], table, ALU.mult)
                last.then_inc(crossed_done, 1)

            def body(chunk, s):
                if kind(chunk) < 2:
                    for t in range(TILES):
                        cross(chunk, t)

            chunks(nc.gpsimd, body)


def attention(nc, ident, table, lens, qT, k_resident, kT_own, v_cache, v_own, oT):
    UNITS = B * HK
    KEYS = L + S
    CH = L // P
    GATHER = HK - 3
    ACTS, DVES = range(GATHER), range(GATHER, 2 * GATHER)
    POOLS = range(2 * GATHER, NPP)
    LEFT = NPP // 2
    BANK = 512
    FROM = BANK - LEFT * PSIZE
    with Scope(nc) as c:
        K = c.sb("at_K", [P, 2, NPP + 1, HK, PSIZE])
        V = c.sb("at_V", [P, 2, CH + 1, HK * DH])
        Q = c.sb("at_Q", [P, 2, HK, P])
        out = c.sb("at_out", [P, 2, HK, P])
        tab = c.sb("at_tab", [1, B * NPP], I32)
        tab_all = c.sb("at_tab_all", [P, B * CH, BPT], I32)
        lane, rows = c.sb("at_lane", [P, 1], I32), c.sb("at_rows", [P, B * CH], I32)
        lanef, rowsf = c.sb("at_lanef", [P, 1]), c.sb("at_rowsf", [P, B * CH])
        rows_slot = c.sb("at_rows_slot", [P, 2, CH], I32)
        lensi, lensf = c.sb("at_lensi", [P, B], I32), c.sb("at_lensf", [P, B])
        keyi, keyf = c.sb("at_keyi", [P, L], I32), c.sb("at_keyf", [P, L])
        mask = c.sb("at_mask", [P, 2, KEYS])
        scores, probs = c.sb("at_scores", [P, 2, KEYS]), c.sb("at_probs", [P, 2, KEYS])
        least = c.sb("at_least", [P, 2])
        total, inverse = c.sb("at_total", [P, 2]), c.sb("at_inverse", [P, 2])
        PT = c.sb("at_PT", [P, 2, CH + 1, P])
        psS = c.ps("at_psS", [P, 2, 2 * BANK])
        psP, psX, psO = c.ps("at_psP", [P, CH, P]), c.ps("at_psX", [P, BANK]), c.ps("at_psO", [P, 2, BANK])

        table_loaded, lens_loaded = c.sem("at_table_loaded"), c.sem("at_lens_loaded")
        counted, prepared = c.sem("at_counted"), c.sem("at_prepared")
        k_loaded = [c.sem(f"at_k_loaded{s}") for s in range(2)]
        v_loaded = [c.sem(f"at_v_loaded{s}") for s in range(2)]
        v_own_loaded = [c.sem(f"at_v_own_loaded{s}") for s in range(2)]
        stored = [c.sem(f"at_stored{s}") for s in range(2)]
        rows_copied, rows_seen = c.sem("at_rows_copied"), c.sem("at_rows_seen")
        scored = c.sem("at_scored")
        scores_seen = c.sem("at_scores_seen")
        masked = c.sem("at_masked")
        mask_made = c.sem("at_mask_made")
        exped = c.sem("at_exped")
        turned = c.sem("at_turned")
        cached_kept, own_kept = c.sem("at_cached_kept"), c.sem("at_own_kept")
        weighted = c.sem("at_weighted")
        constants, inverted = c.sem("at_constants"), c.sem("at_inverted")
        normed = c.sem("at_normed")
        out_kept = c.sem("at_out_kept")
        k_act, k_dve, k_pool = c.sem("at_k_act"), c.sem("at_k_dve"), c.sem("at_k_pool")
        block = c.block()

        def known(b):
            return isinstance(b, int)

        def batches(eng, body):
            for b in range(2):
                body(b, b)
            with eng.Fori(1, B // 2 - 2) as i:
                for s in range(2):
                    body(i * 2 + s, s)
            for b in range(B - 4, B):
                body(b, b % 2)

        def exists(b, h):
            return not known(b) or 0 <= b * HK + h < UNITS

        def at(b, s, h):
            return b + h // HK, (s + h // HK) % 2, h % HK

        def wait_loads(eng, sem, b, s, n):
            eng.wait_ge(sem, (b // 2 + 1) * (16 * n) if known(b) else (b - s) * (8 * n) + 16 * n)

        def gather(eng, move, b, s, n, sem):
            page = eng.value_load(tab[0:1, ds(b * NPP + n, 1)], min_val=0, max_val=PAGES - 1)
            move(K[:, s, n, :, :], k_resident[:, ds(page, 1), :, :]).then_inc(sem, 1)

        def wait_slot(eng, b):
            if not known(b) or b >= 2:
                eng.wait_ge(scored, b * HK - HK)

        @block.sync
        def _(sp):
            lens_row = lens.rearrange("(a b) -> a b", a=1)
            table_row = table.rearrange("(a b) n -> a (b n)", a=1)
            sp.dma_start(tab[:], table_row).then_inc(table_loaded, 16)
            sp.dma_start(tab_all[:].rearrange("p c j -> p (c j)"),
                         table_row.broadcast_to([P, B * NPP])).then_inc(table_loaded, 16)
            sp.dma_start(lensi[:], lens_row.broadcast_to([P, B])).then_inc(lens_loaded, 16)

            def load_keys(b, s):
                sp.dma_start(Q[:, s, :, :], qT[b]).then_inc(k_loaded[s], 16)
                sp.dma_start(K[:, s, NPP, :, :].rearrange("d h k -> d (h k)").rearrange("d (c m) -> d c m", c=2),
                             kT_own[b]).then_inc(k_loaded[s], 16)

            def load_own_values(b, s):
                sp.dma_start(V[0:S, s, CH, :], v_own[b]).then_inc(v_own_loaded[s], 16)

            for b in range(2):
                load_keys(b, b)
                load_own_values(b, b)

            def body(b, s):
                if not known(b) or b + 2 < B:
                    sp.wait_ge(scored, b * HK + HK)
                    load_keys(b + 2, s)
                    sp.wait_ge(weighted, b * HK + HK)
                    load_own_values(b + 2, s)
                sp.wait_ge(out_kept, b * HK + HK)
                sp.dma_start(oT[b], out[:, s, :, :].rearrange("d h m -> d (h m)")).then_inc(stored[s], 16)

            batches(nc.sync, body)
            for s in range(2):
                sp.wait_ge(stored[s], 16 * (B // 2))

        @block.gpsimd
        def _(pool):
            nc.gpsimd.iota(keyi[:], pattern=[[1, L]], base=0, channel_multiplier=0).then_inc(counted, 1)
            for j in range(BPT):
                pool.wait_ge(counted, j + 1)
                nc.gpsimd.iota(lane[j * S:(j + 1) * S, :], pattern=[[0, 1]], base=0,
                               channel_multiplier=1).then_inc(counted, 1)
            pool.wait_ge(prepared, 1)
            v_rows = v_cache.rearrange("a k h d -> (a k) (h d)")

            def load_values(b, s):
                nc.gpsimd.tensor_copy(rows_slot[:, s, :], rows[:, ds(b * CH, CH)]).then_inc(rows_copied, 1)
                pool.wait_ge(rows_copied, b + 1)
                pool.sem_inc(rows_seen, 1)
                for n in range(CH):
                    pool.indirect_dma_start(
                        out=V[:, s, n, :], out_offset=None, in_=v_rows,
                        in_offset=bass.IndirectOffsetOnAxis(ap=rows_slot[:, s, n:n + 1], axis=0),
                    ).then_inc(v_loaded[s], 16)

            def keys(b, s):
                wait_slot(pool, b)
                for n in POOLS:
                    gather(pool, nc.gpsimd.tensor_copy, b, s, n, k_pool)

            keys(0, 0)
            for b in range(2):
                load_values(b, b)

            def body(b, s):
                if exists(b + 1, 0):
                    keys(b + 1, 1 - s)
                if not known(b) or b + 2 < B:
                    pool.wait_ge(weighted, b * HK + HK)
                    wait_loads(pool, v_loaded[s], b, s, CH)
                    load_values(b + 2, s)

            batches(nc.gpsimd, body)

        @block.tensor
        def _(pe):
            def score(b, s, h):
                unit = b * HK + h
                if h == 0:
                    wait_loads(pe, k_loaded[s], b, s, 2)
                    for sem, pages in ((k_act, ACTS), (k_dve, DVES), (k_pool, POOLS)):
                        pe.wait_ge(sem, b * len(pages) + len(pages))
                if not known(b) or unit >= 2:
                    pe.wait_ge(masked, unit - 1)
                for start, pages in ((FROM, slice(0, LEFT)), (BANK, slice(LEFT, NPP + 1))):
                    part = psS[:, h % 2, start:start + (pages.stop - pages.start) * PSIZE]
                    last = nc.tensor.matmul(part.rearrange("p (n k) -> p n k", k=PSIZE), Q[:, s, h, :],
                                            K[:, s, pages, h, :], start=True, stop=True)
                last.then_inc(scored, 1)

            def turn(b, h):
                unit = b * HK + h
                pe.wait_ge(normed, unit + 1)
                if not known(b) or unit >= 1:
                    pe.wait_ge(cached_kept, unit)
                    pe.wait_ge(own_kept, unit)
                for n in range(CH):
                    nc.tensor.transpose(psP[:, n, :], probs[:, h % 2, n * P:(n + 1) * P], ident[:])
                nc.tensor.transpose(psX[0:S, 0:P], probs[:, h % 2, L:KEYS], ident[:]).then_inc(turned, 1)

            def weigh_start(b, s, h):
                unit = b * HK + h
                if h == 0:
                    wait_loads(pe, v_loaded[s], b, s, CH)
                    wait_loads(pe, v_own_loaded[s], b, s, 1)
                pe.wait_ge(cached_kept, unit + 1)
                if not known(b) or unit >= 2:
                    pe.wait_ge(out_kept, unit - 1)
                for n in range(CH // 2):
                    nc.tensor.matmul(psO[:, h % 2, 0:P], V[:, s, n, h * DH:(h + 1) * DH], PT[:, h % 2, n, :],
                                     start=n == 0, stop=False)

            def weigh_end(b, s, h):
                for n in range(CH // 2, CH):
                    nc.tensor.matmul(psO[:, h % 2, 0:P], V[:, s, n, h * DH:(h + 1) * DH], PT[:, h % 2, n, :],
                                     start=False, stop=False)
                pe.wait_ge(own_kept, b * HK + h + 1)
                nc.tensor.matmul(psO[:, h % 2, 0:P], V[0:S, s, CH, h * DH:(h + 1) * DH], PT[0:S, h % 2, CH, :],
                                 start=False, stop=True).then_inc(weighted, 1)

            score(0, 0, 0)
            score(0, 0, 1)
            turn(0, 0)

            def body(b, s):
                for h in range(HK):
                    if exists(b, h + 2):
                        score(*at(b, s, h + 2))
                    weigh_start(b, s, h)
                    if exists(b, h + 1):
                        turn(b, h + 1)
                    weigh_end(b, s, h)

            batches(nc.tensor, body)

        @block.vector
        def _(dve):
            dve.wait_ge(lens_loaded, 16)
            dve.wait_ge(table_loaded, 32)
            dve.wait_ge(counted, 1 + BPT)
            nc.vector.tensor_copy(lensf[:], lensi[:])
            nc.vector.tensor_copy(keyf[:], keyi[:])
            nc.vector.tensor_copy(lanef[:], lane[:])
            for j in range(BPT):
                nc.vector.tensor_copy(rowsf[j * S:(j + 1) * S, :], tab_all[j * S:(j + 1) * S, :, j])
            nc.vector.memset(mask[:], 0.0).then_inc(constants, 1)
            dve.wait_ge(constants, 1)
            nc.vector.tensor_scalar(rows[:], rowsf[:], float(PSIZE), lanef[:, 0:1], ALU.mult,
                                    ALU.add).then_inc(prepared, 1)

            def mask_scores(b, s, h):
                unit = b * HK + h
                if h == 0:
                    nc.vector.tensor_scalar(mask[:, s, 0:L], keyf[:], lensf[:, ds(b, 1)], MASKED, ALU.is_ge,
                                            ALU.mult).then_inc(mask_made, 1)
                    dve.wait_ge(mask_made, b + 1)
                dve.wait_ge(scored, unit + 1)
                dve.sem_inc(scores_seen, 1)
                nc.vector.tensor_tensor_reduce(out=scores[:, h % 2, :], in0=psS[:, h % 2, FROM:FROM + KEYS],
                                               in1=mask[:, s, :], scale=-SCALE, scalar=-MASKED, op0=ALU.add,
                                               op1=ALU.min, accum_out=least[:, h % 2:h % 2 + 1]).then_inc(masked, 1)

            def keep_own(b, h):
                unit = b * HK + h
                dve.wait_ge(turned, unit + 1)
                if not known(b) or unit >= 2:
                    dve.wait_ge(weighted, unit - 1)
                nc.vector.tensor_copy(PT[0:S, h % 2, CH, :], psX[0:S, 0:P]).then_inc(own_kept, 1)

            def keep_out(b, s, h):
                dve.wait_ge(weighted, b * HK + h + 1)
                if h == 0 and (not known(b) or b >= 2):
                    dve.wait_ge(stored[s], (b // 2) * 16 if known(b) else (b - s) * 8)
                nc.vector.tensor_copy(out[:, s, h, :], psO[:, h % 2, 0:P]).then_inc(out_kept, 1)

            def normalise(b, h):
                unit, r = b * HK + h, h % 2
                dve.wait_ge(exped, unit + 1)
                nc.vector.reciprocal(inverse[:, r:r + 1], total[:, r:r + 1]).then_inc(inverted, 1)
                dve.wait_ge(inverted, unit + 1)
                nc.vector.tensor_scalar(probs[:, r, :], probs[:, r, :], inverse[:, r:r + 1], None,
                                        ALU.mult).then_inc(normed, 1)

            for n in DVES:
                gather(dve, nc.vector.tensor_copy, 0, 0, n, k_dve)
            mask_scores(0, 0, 0)
            normalise(0, 0)
            mask_scores(0, 0, 1)
            keep_own(0, 0)

            def body(b, s):
                for h in range(HK):
                    if exists(b, h + 1):
                        normalise(b, h + 1)
                    if exists(b, h + 2):
                        mask_scores(*at(b, s, h + 2))
                    if exists(b, h - 1):
                        keep_out(*at(b, s, h - 1))
                    if exists(b, h + 1):
                        keep_own(b, h + 1)
                    if h < GATHER and exists(b + 1, 0):
                        if h == 0:
                            wait_slot(dve, b + 1)
                        gather(dve, nc.vector.tensor_copy, b + 1, 1 - s, DVES[h], k_dve)

            batches(nc.vector, body)
            keep_out(B - 1, (B - 1) % 2, HK - 1)

        @block.scalar
        def _(act):
            def exp(b, h):
                unit = b * HK + h
                act.wait_ge(masked, unit + 1)
                if not known(b) or unit >= 2:
                    act.wait_ge(turned, unit - 1)
                nc.scalar.activation(probs[:, h % 2, :], scores[:, h % 2, :], ACT.Exp,
                                     bias=least[:, h % 2:h % 2 + 1], scale=-1.0,
                                     accum_out=total[:, h % 2:h % 2 + 1]).then_inc(exped, 1)

            def keep_cached(b, h):
                unit = b * HK + h
                act.wait_ge(turned, unit + 1)
                if not known(b) or unit >= 2:
                    act.wait_ge(weighted, unit - 1)
                nc.scalar.copy(PT[:, h % 2, 0:CH, :], psP[:]).then_inc(cached_kept, 1)

            act.wait_ge(table_loaded, 32)
            for n in ACTS:
                gather(act, nc.scalar.copy, 0, 0, n, k_act)
            exp(0, 0)
            keep_cached(0, 0)
            exp(0, 1)

            def body(b, s):
                for h in range(HK):
                    if exists(b, h + 2):
                        exp(b, h + 2)
                    if exists(b, h + 1):
                        keep_cached(b, h + 1)
                    if h < GATHER and exists(b + 1, 0):
                        if h == 0:
                            wait_slot(act, b + 1)
                        gather(act, nc.scalar.copy, b + 1, 1 - s, ACTS[h], k_act)

            batches(nc.scalar, body)


def output_layer(nc, ident, Wo, oT, x_in, result):
    HALF = HQ // 2
    BLOCKS = HQ * DH // D
    with Scope(nc) as c:
        WH, WL = c.sb("ol_WH", [P, HQ, D], F32R), c.sb("ol_WL", [P, HQ, D], F32R)

        with Scope(nc) as w:
            nat = w.sb("ol_nat", [P, 2, KC, D])
            ps = w.ps("ol_psW", [P, 2, KC, D])
            loaded = [w.sem(f"ol_w_loaded{s}") for s in range(2)]
            turned, high, low = w.sem("ol_w_turned"), w.sem("ol_w_high"), w.sem("ol_w_low")
            blocks = Wo.rearrange("(o p) (a k) -> a p o k", p=P, k=D)
            block = w.block()

            @block.sync
            def _(sp):
                for a in range(BLOCKS):
                    if a >= 2:
                        sp.wait_ge(turned, a - 1)
                    sp.dma_start(nat[:, a % 2, :, :], blocks[a]).then_inc(loaded[a % 2], 16)

            @block.tensor
            def _(pe):
                pe.sem_inc(low, 2)
                with nc.tensor.Fori(0, BLOCKS // 2) as i:
                    for s in range(2):
                        pe.wait_ge(loaded[s], i * 16 + 16)
                        pe.wait_ge(low, i * 2 + (s + 1))
                        for k in range(KC):
                            for o in range(KC):
                                last = nc.tensor.transpose(ps[:, s, k, o * P:(o + 1) * P],
                                                           nat[:, s, o, k * P:(k + 1) * P], ident[:])
                        last.then_inc(turned, 1)

            @block.scalar
            def _(act):
                with nc.scalar.Fori(0, BLOCKS // 2) as i:
                    for s in range(2):
                        act.wait_ge(turned, i * 2 + (s + 1))
                        nc.scalar.copy(WH[:, ds(i * (2 * KC) + s * KC, KC), :], ps[:, s, :, :]).then_inc(high, 1)

            @block.vector
            def _(dve):
                with nc.vector.Fori(0, BLOCKS // 2) as i:
                    for s in range(2):
                        heads = ds(i * (2 * KC) + s * KC, KC)
                        dve.wait_ge(high, i * 2 + (s + 1))
                        nc.vector.tensor_tensor(WL[:, heads, :], ps[:, s, :, :], WH[:, heads, :].bitcast(F32),
                                                ALU.subtract).then_inc(low, 1)

        with Scope(nc) as w:
            o = w.sb("ol_o", [P, 2, BPT, HALF, S])
            OH, OL = w.sb("ol_OH", [P, 2, HALF, P], F32R), w.sb("ol_OL", [P, 2, HALF, P], F32R)
            x_row, y_row = w.sb("ol_x_row", [P, 2, D]), w.sb("ol_y_row", [P, 2, D])
            ps = w.ps("ol_ps", [P, 2, D])
            loaded = [w.sem(f"ol_loaded{s}") for s in range(2)]
            x_loaded = [w.sem(f"ol_x_loaded{s}") for s in range(2)]
            stored = [w.sem(f"ol_stored{s}") for s in range(2)]
            high, low, done, added = (w.sem(f"ol_{x}") for x in ("high", "low", "done", "added"))
            block = w.block()

            @block.sync
            def _(sp):
                def load(t, half):
                    sp.dma_start(o[:, half, :, :, :].rearrange("d j h s -> d j (h s)"),
                                 oT[ds(t * BPT, BPT), :, half * HALF * S:(half + 1) * HALF * S]
                                 .rearrange("j d m -> d j m")).then_inc(loaded[half], 16)

                def load_x(t, r):
                    sp.dma_start(x_row[:, r, :], x_in[t]).then_inc(x_loaded[r], 16)

                def store(t, r):
                    sp.wait_ge(added, t + 1)
                    sp.dma_start(result[t], y_row[:, r, :]).then_inc(stored[r], 16)

                for r in range(2):
                    sp.sem_inc(stored[r], 16)
                load(0, 0)
                load(0, 1)
                load_x(0, 0)
                load_x(1, 1)
                with nc.sync.Fori(0, TILES // 2 - 1) as i:
                    for r in range(2):
                        t = i * 2 + r
                        for half in range(2):
                            sp.wait_ge(low, t * 2 + (half + 1))
                            load(t + 1, half)
                        store(t, r)
                        load_x(t + 2, r)
                for half in range(2):
                    sp.wait_ge(low, TILES * 2 - 3 + half)
                    load(TILES - 1, half)
                for r in range(2):
                    store(TILES - 2 + r, r)
                for r in range(2):
                    sp.wait_ge(stored[r], 16 * (TILES // 2 + 1))

            @block.scalar
            def _(act):
                act.sem_inc(done, 2)
                with nc.scalar.Fori(0, TILES) as t:
                    for half in range(2):
                        act.wait_ge(loaded[half], t * 16 + 16)
                        act.wait_ge(done, t * 2 + (half + 1))
                        nc.scalar.copy(OH[:, half, :, :].rearrange("d h (j s) -> d j h s", j=BPT),
                                       o[:, half, :, :, :]).then_inc(high, 1)

            @block.vector
            def _(dve):
                def low_parts(t):
                    for half in range(2):
                        dve.wait_ge(high, t * 2 + (half + 1))
                        dve.wait_ge(done, t * 2 + (half + 1))
                        nc.vector.tensor_tensor(
                            OL[:, half, :, :].rearrange("d h (j s) -> d j h s", j=BPT), o[:, half, :, :, :],
                            OH[:, half, :, :].bitcast(F32).rearrange("d h (j s) -> d j h s", j=BPT),
                            ALU.subtract).then_inc(low, 1)

                def add(t, i, r):
                    dve.wait_ge(done, t * 2 + 4)
                    dve.wait_ge(x_loaded[r], i * 16 + 16)
                    dve.wait_ge(stored[r], i * 16 + 16)
                    nc.vector.tensor_tensor(y_row[:, r, :], ps[:, r, :], x_row[:, r, :],
                                            ALU.add).then_inc(added, 1)

                low_parts(0)
                with nc.vector.Fori(0, TILES // 2 - 1) as i:
                    for r in range(2):
                        low_parts(i * 2 + (r + 1))
                        add(i * 2 + r, i, r)
                low_parts(TILES - 1)
                for r in range(2):
                    add(TILES - 2 + r, TILES // 2 - 1, r)

            @block.tensor
            def _(pe):
                def products(t, r, first):
                    if not first:
                        pe.wait_ge(added, t - 1)
                    for half in range(2):
                        pe.wait_ge(low, t * 2 + (half + 1))
                        for h in range(HALF):
                            for n, (x, wt) in enumerate(((OH, WH), (OH, WL), (OL, WH))):
                                last = nc.tensor.matmul(ps[:, r, :], x[:, half, h, :], wt[:, half * HALF + h, :],
                                                        start=half == 0 and h == 0 and n == 0,
                                                        stop=half == 1 and h == HALF - 1 and n == 2)
                        last.then_inc(done, 1)

                products(0, 0, True)
                products(1, 1, True)
                with nc.tensor.Fori(1, TILES // 2) as i:
                    for r in range(2):
                        products(i * 2 + r, r, False)


def build(nc, x, ids0, ids1, ids2, table, lens, w0, W, Wr, A, Bm, w2, Wq, Wk, Wv, Wo, q_norm_w, k_norm_w,
          k_cache, v_cache, out):
    def dram(name, shape):
        return nc.dram_tensor(name, shape, F32, kind="Internal").ap()

    x_tiles = x.rearrange("(t j) s d -> t (j s) d", j=BPT)
    out_tiles = out.rearrange("(t j) s d -> t (j s) d", j=BPT)
    x1, x2, x3 = (dram(f"x{n}", [TILES, P, D]) for n in (1, 2, 3))
    qT = dram("qT", [B, DH, HK, P])
    kT_own = dram("kT_own", [B, DH, 2, P])
    v_own = dram("v_own", [TILES, P, 2, D])
    oT = dram("oT", [B, DH, HQ * S])

    with Scope(nc) as whole:
        ident = whole.sb("ident", [P, P])
        identity(nc, ident)
        with Scope(nc) as c:
            XT = c.sb("XT", [P, TILES, KC, P])
            load_x(nc, x, ident, XT)
            adapter_layer(nc, ident, "l0", w0, ids0, w0.shape[0], x_tiles, x1, XT)
            expert_layer(nc, ident, W, Wr, A, Bm, ids1, x1, x2, XT)
            straight, crossed = (c.sb(name, [P, 2, TILES, 2, DH // 2]) for name in ("straight", "crossed"))
            adapter_layer(nc, ident, "l2", w2, ids2, w2.shape[0], x2, x3, XT,
                          beside=lambda scope: rope_tables(nc, scope, lens, q_norm_w, k_norm_w, straight, crossed))
            XH, XL = (c.sb(name, [P, TILES, KC, P], F32R) for name in ("XH", "XL"))
            project(nc, ident, XT, XH, XL, straight, crossed, Wq, Wk, Wv, qT, kT_own, v_own)
        with Scope(nc) as c:
            k_resident = c.sb("k_resident", [P, PAGES, HK, PSIZE])
            cache_keys(nc, ident, k_cache, k_resident)
            attention(nc, ident, table, lens, qT, k_resident, kT_own, v_cache,
                      v_own.rearrange("t (j s) c m -> (t j) s (c m)", j=BPT), oT)
        output_layer(nc, ident, Wo, oT, x3, out_tiles)


INPUTS = ["x", "itok_B_1_14", "itok_B_0_7", "itok_B_3_7", "itok_Bx16_0_63", "itok_B_207_1644", "L0_cond_weight",
          "L1_cond_W", "L1_cond_Wr", "L1_cond_A", "L1_cond_B", "L2_cond_weight", "L3_cond_Wq", "L3_cond_Wk",
          "L3_cond_Wv", "L3_cond_Wo", "L3_cond_q_norm_w", "L3_cond_k_norm_w", "L3_cond_k_cache",
          "L3_cond_v_cache"]


def kernel(**inputs):
    import concourse.bacc as bacc
    from concourse.bass_utils import run_bass_kernel_spmd

    nc = bacc.Bacc("TRN2", target_bir_lowering=False, num_devices=1)
    arrays, args = {}, []
    for name in INPUTS:
        a = np.ascontiguousarray(inputs[name])
        arrays[f"in_{name}"] = a
        args.append(nc.dram_tensor(f"in_{name}", a.shape, mybir.dt.from_np(a.dtype), kind="ExternalInput").ap())
    args.append(nc.dram_tensor("out", (B, S, D), F32, kind="ExternalOutput").ap())
    build(nc, *args)
    return run_bass_kernel_spmd(nc, [arrays], core_ids=[0]).results[0]["out"]
```
